# Optimizing a Trainium2 kernel written in Bass

```python
import numpy as np
import jax
import jax.numpy as jnp

def _softmax(x, axis=-1):
    return jax.nn.softmax(x, axis=axis)

def _gelu(x):
    return jax.nn.gelu(x, approximate=True)

def _silu(x):
    return jax.nn.silu(x)

def _sigmoid(x):
    return jax.nn.sigmoid(x)

def _layernorm(x, axis=-1, eps=1e-05):
    m = jnp.mean(x, axis=axis, keepdims=True)
    v = jnp.var(x, axis=axis, keepdims=True)
    return (x - m) / jnp.sqrt(v + eps)

def _scatter_add(tgt, idx, src, axis=0):
    return tgt.at[idx].add(src)

def _segment_sum(src, seg, n):
    return jax.ops.segment_sum(src, seg, n)
kernel_name = 'mk_flamingo_gated_d1_seqx_r4_370548'

def setup_inputs(seed: int=0):
    np.random.seed(seed)
    _w = jnp.asarray

    def _rec_inputs():
        import jax
        import jax.numpy as jnp
        _rk = jax.random.key(seed)
        x = -0.0003929 + 0.9999 * jax.random.normal(jax.random.fold_in(_rk, 1), (4, 1024, 256), jnp.float32)
        _lenS = 1024 - jax.random.randint(jax.random.fold_in(_rk, 7), (4,), 0, max(1, 1024 // 4) + 1, jnp.int32)
        _lenS2 = 154 - jax.random.randint(jax.random.fold_in(_rk, 8), (4,), 0, max(1, 154 // 4) + 1, jnp.int32)
        _ctx_1024P = jax.random.normal(jax.random.fold_in(_rk, 11), (4, 16, 256), jnp.float32)
        _ctx_1024c = jax.random.dirichlet(jax.random.fold_in(_rk, 511), 0.3 * jnp.ones((16,), jnp.float32), (4, 154))
        _ctx_1024t = jnp.einsum('bsk,bkd->bsd', _ctx_1024c, _ctx_1024P)
        _ctx_1024t = _ctx_1024t * jax.lax.rsqrt(jnp.mean(jnp.square(_ctx_1024t)) + 1e-12) * 0.953939
        ctx_1024 = 2.81802e-05 + 1.00001 * (_ctx_1024t + 0.3 * jax.random.normal(jax.random.fold_in(_rk, 611), (4, 154, 256), jnp.float32))
        _validS = jnp.arange(1024)[None, :] < _lenS[:, None]
        _validS2 = jnp.arange(154)[None, :] < _lenS2[:, None]
        _causal = jnp.tril(jnp.ones((1024, 1024), dtype=bool))
        mask_BxS2_ik0 = jnp.where(jnp.broadcast_to(_validS2[:, :], (4, 154)), 0, 1).astype(jnp.int32)
        _g = jax.random.normal(jax.random.fold_in(_rk, 9001), (2, 1), jnp.float32)
        _g = jnp.sign(_g) * jnp.maximum(jnp.abs(_g), 1.0) + (_g == 0) * 1.0
        g_xattn = _g[0]
        g_ffn = _g[1]
        return (x, ctx_1024, mask_BxS2_ik0, g_xattn, g_ffn)
    x, ctx_1024, mask_BxS2_ik0, g_xattn, g_ffn = _rec_inputs()

    def _L0_xattn_setup():
        import jax, jax.numpy as jnp
        import numpy as np
        D = 256
        NEG = -1000000000.0
        key = jax.random.key(seed)
        ks = jax.random.split(key, 9)
        B, Lq, Lk, d = (8, 512, 512, D)
        s = 1.0 / np.sqrt(d)
        return {'hm_tokens': jax.random.normal(ks[0], (B, Lq, d), jnp.float32), 'text_tokens': jax.random.normal(ks[1], (B, Lk, d), jnp.float32), 'text_mask': jax.random.randint(ks[2], (B, Lk), 0, 2, jnp.int32), 'Wq': jax.random.normal(ks[3], (d, d), jnp.float32) * s, 'bq': jnp.zeros((d,), jnp.float32), 'Wk': jax.random.normal(ks[4], (d, d), jnp.float32) * s, 'bk': jnp.zeros((d,), jnp.float32), 'Wv': jax.random.normal(ks[5], (d, d), jnp.float32) * s, 'bv': jnp.zeros((d,), jnp.float32)}
    _L0_xattn_all = _L0_xattn_setup()
    _L0_xattn_in = {k: v for k, v in _L0_xattn_all.items() if k in ('Wq', 'bq', 'Wk', 'bk', 'Wv', 'bv')}
    del _L0_xattn_all

    def _L0_ffn_setup():
        import jax, jax.numpy as jnp
        import numpy as np
        B, L, D, E, K, DFF = (2, 512, 256, 8, 2, 1024)
        key = jax.random.key(seed)
        kx, kr, kg, ku, kd = jax.random.split(key, 5)
        scale = 0.02
        return {'x': jax.random.normal(kx, (B, L, D), dtype=jnp.float32), 'Wr': jax.random.normal(kr, (E, D), dtype=jnp.float32) * scale, 'Wg': jax.random.normal(kg, (E, DFF, D), dtype=jnp.float32) * scale, 'Wu': jax.random.normal(ku, (E, DFF, D), dtype=jnp.float32) * scale, 'Wd': jax.random.normal(kd, (E, D, DFF), dtype=jnp.float32) * scale}
    _L0_ffn_all = _L0_ffn_setup()
    _L0_ffn_in = {k: v for k, v in _L0_ffn_all.items() if k in ('Wr', 'Wg', 'Wu', 'Wd')}
    del _L0_ffn_all
    return {'x': x, 'ctx_1024': ctx_1024, 'mask_BxS2_ik0': mask_BxS2_ik0, 'g_xattn': g_xattn, 'g_ffn': g_ffn, 'L0_xattn_Wq': _L0_xattn_in['Wq'], 'L0_xattn_bq': _L0_xattn_in['bq'], 'L0_xattn_Wk': _L0_xattn_in['Wk'], 'L0_xattn_bk': _L0_xattn_in['bk'], 'L0_xattn_Wv': _L0_xattn_in['Wv'], 'L0_xattn_bv': _L0_xattn_in['bv'], 'L0_ffn_Wr': _L0_ffn_in['Wr'], 'L0_ffn_Wg': _L0_ffn_in['Wg'], 'L0_ffn_Wu': _L0_ffn_in['Wu'], 'L0_ffn_Wd': _L0_ffn_in['Wd']}

def reference(x, ctx_1024, mask_BxS2_ik0, g_xattn, g_ffn, L0_xattn_Wq, L0_xattn_bq, L0_xattn_Wk, L0_xattn_bk, L0_xattn_Wv, L0_xattn_bv, L0_ffn_Wr, L0_ffn_Wg, L0_ffn_Wu, L0_ffn_Wd):
    import jax
    import jax.numpy as jnp

    def _L0_xattn_ref(hm_tokens, text_tokens, text_mask, Wq, bq, Wk, bk, Wv, bv):
        import jax, jax.numpy as jnp
        import numpy as np
        D = 256
        NEG = -1000000000.0
        d = hm_tokens.shape[-1]
        Q = hm_tokens @ Wq + bq
        K = text_tokens @ Wk + bk
        V = text_tokens @ Wv + bv
        scores = jnp.einsum('bqd,bkd->bqk', Q, K) / jnp.sqrt(jnp.float32(d))
        scores = jnp.where(text_mask[:, None, :] == 0, jnp.float32(NEG), scores)
        attn = jax.nn.softmax(scores, axis=-1)
        return jnp.einsum('bqk,bkd->bqd', attn, V)

    def _L0_ffn_ref(x, Wr, Wg, Wu, Wd):
        import jax, jax.numpy as jnp
        import numpy as np
        B, L, D, E, K, DFF = (2, 512, 256, 8, 2, 1024)
        Bb, Ll, Dd = x.shape
        T = Bb * Ll
        xt = x.reshape(T, Dd)
        logits = jnp.einsum('td,ed->te', xt, Wr)
        scores = jax.nn.softmax(logits, axis=-1)
        k_scores, k_ids = jax.lax.top_k(scores, K)
        eps = jnp.finfo(x.dtype).eps
        k_w = k_scores / (k_scores.sum(axis=-1, keepdims=True) + eps)
        combine = jnp.sum(jax.nn.one_hot(k_ids, E, dtype=x.dtype) * k_w[..., None], axis=1)
        g = jnp.einsum('td,efd->etf', xt, Wg)
        u = jnp.einsum('td,efd->etf', xt, Wu)
        h = jax.nn.relu(g) * u
        out_e = jnp.einsum('etf,edf->etd', h, Wd)
        out = jnp.einsum('te,etd->td', combine, out_e)
        return out.reshape(Bb, Ll, Dd)
    x = x + jnp.tanh(g_xattn[0]) * _L0_xattn_ref(_layernorm(x, axis=-1), ctx_1024, mask_BxS2_ik0, L0_xattn_Wq, L0_xattn_bq, L0_xattn_Wk, L0_xattn_bk, L0_xattn_Wv, L0_xattn_bv)
    x = x + jnp.tanh(g_ffn[0]) * _L0_ffn_ref(_layernorm(x, axis=-1), L0_ffn_Wr, L0_ffn_Wg, L0_ffn_Wu, L0_ffn_Wd)
    return x

_drawn_inputs = setup_inputs


def setup_inputs(seed=0):
    import zlib

    import numpy as np

    out = dict(_drawn_inputs(seed))
    spreads = {'L0_xattn_bq': (0.0, 0.311), 'L0_xattn_bk': (0.0, 0.8), 'L0_xattn_bv': (0.0, 0.1)}
    factors = {}
    for name, (base, spread) in spreads.items():
        noise = np.random.default_rng([zlib.crc32(name.encode()), seed]).standard_normal(out[name].shape)
        drawn = base * np.exp(spread * noise) if base else spread * noise
        out[name] = jnp.asarray(drawn.astype(out[name].dtype))
    for name, factor in factors.items():
        out[name] = (out[name] * factor).astype(out[name].dtype)
    return out
```

```python
from contextlib import ExitStack

import concourse.bass as bass
from concourse import mybir

ALU = mybir.AluOpType
ACT = mybir.ActivationFunctionType
AX = mybir.AxisListType
F32 = mybir.dt.float32
F32R = mybir.dt.float32r
BF16 = mybir.dt.bfloat16
I32 = mybir.dt.int32

P = 128
NB, S, D = 4, 1024, 256
T = NB * S
LC = 154
CH = LC // 2
KC = D // P
NT = S // P
TQ = NT // 2
E, F = 8, 1024
FC = F // P
FH = F // 2
WCOLS = 2 * KC * F + FC * D
PIECE = 1024
PIECES = WCOLS // PIECE
MIN_BLOCKS = 4
PAD = MIN_BLOCKS * P
REGION = T + PAD
ROW = D + 2 * E
LN_EPS = 1e-5
K_EPS = 2.0 ** -23
MASKED = -1e9 * 16.0
BELOW = -1e30


class Steps:

    def __init__(self, engine, sem):
        self.engine, self.sem, self.base, self.n = engine, sem, 0, 0

    def mark(self, ins):
        ins.then_inc(self.sem, 1)
        self.n += 1

    def settle(self):
        self.engine.wait_ge(self.sem, self.base + self.n)

    def loop(self, i, per):
        self.base, self.per, self.entry = self.n + i * per, per, self.n
        self.n = 0

    def leave(self, turns):
        assert self.n == self.per, (self.n, self.per)
        self.base, self.n = 0, self.entry + turns * self.per


def build(nc, x, ctx_t, w_small, mask, bq, bk, bv, gates, wr_t, w_experts, out):
    rows_dram = nc.dram_tensor("rows_by_expert", [E * REGION, ROW], F32).ap()

    with ExitStack() as whole:
        def sb(name, shape, dt, stack=whole):
            return stack.enter_context(nc.sbuf_tensor(name, shape, dt))

        def sem(name):
            return whole.enter_context(nc.semaphore(name))

        ps = whole.enter_context(nc.psum_tensor("ps", [P, 8, 512], F32))

        w_raw = sb("w_raw", [P, WCOLS], F32)
        w_hi = [sb("w_hi0", [P, WCOLS], F32R)]
        w_lo = [sb("w_lo0", [P, WCOLS], F32R)]
        ident = sb("ident", [P, P], F32)
        earlier = sb("earlier", [P, P], BF16)
        ones = sb("ones", [P, P], BF16)
        gate = sb("gate", [P, 2], F32)
        count_row = sb("count_row", [P, E], I32)
        last_row = sb("last_row", [P, E], I32)
        first_row = sb("first_row", [P, E], I32)
        pads = sb("pads", [P, MIN_BLOCKS, ROW], F32)

        att = ExitStack()
        xb = sb("xb", [P, NT, D], F32, att)
        xn = sb("xn", [P, NT, D], F32, att)
        t_hi = [sb(f"t_hi{q}", [P, KC, TQ * P], F32R, att) for q in range(2)]
        t_lo = [sb(f"t_lo{q}", [P, KC, TQ * P], F32R, att) for q in range(2)]
        m_hi = sb("m_hi", [P, KC * NB * LC], F32R, att)
        m_lo = sb("m_lo", [P, KC * NB * LC], F32R, att)
        v_hi = sb("v_hi", [P, NB * 2 * D], F32R, att)
        v_lo = sb("v_lo", [P, NB * 2 * D], F32R, att)
        wr_f = sb("wr_f", [P, KC, E], F32, att)
        wr_hi = sb("wr_hi", [P, KC, E], F32R, att)
        wr_lo = sb("wr_lo", [P, KC, E], F32R, att)
        bias_all = sb("bias_all", [P, NB * LC], F32, att)
        bias_now = sb("bias_now", [P, LC], F32, att)
        gate_in = sb("gate_in", [P, 2], F32, att)
        iota_i = sb("iota_i", [P, 2, E], I32, att)
        falling = sb("falling", [P, E], F32, att)
        region0 = sb("region0", [P, E], F32, att)
        stats = sb("stats", [P, NT, 6], F32, att)
        moments = sb("moments", [P, NT, 2], F32, att)
        ln_v = sb("ln_v", [P, NT], F32, att)
        ln_l = sb("ln_l", [P, NT], F32, att)
        ln_y = sb("ln_y", [P, NT], F32, att)
        ln_a = sb("ln_a", [P, NT], F32, att)
        ln_b = sb("ln_b", [P, NT], F32, att)
        rstd = sb("rstd", [P, NT], F32, att)
        neg_max = sb("neg_max", [P, NT], F32, att)
        exp_sum = sb("exp_sum", [P, NT], F32, att)
        exp_inv = sb("exp_inv", [P, NT], F32, att)
        att_scale = sb("att_scale", [P, NT], F32, att)
        below = sb("below", [P, NT, E], F32, att)
        ex = sb("ex", [P, NT, E], F32, att)
        cand = sb("cand", [P, NT, E], F32, att)
        best = sb("best", [P, NT], F32, att)
        second = sb("second", [P, NT], F32, att)
        ratio = sb("ratio", [P, NT], F32, att)
        chosen = sb("chosen", [P, 2, NT, E], F32, att)
        slot_of = sb("slot_of", [P, 2, NT, E], F32, att)
        place = sb("place", [P, NT, E], F32, att)
        e_sum = sb("e_sum", [P, NT], F32, att)
        den = sb("den", [P, NT], F32, att)
        w_first = sb("w_first", [P, NT], F32, att)
        w_second = sb("w_second", [P, NT], F32, att)
        picked = sb("picked", [P, NT, E], BF16, att)
        picked_before = sb("picked_before", [P, E], BF16, att)
        picked_now = sb("picked_now", [P, E], F32, att)
        slots = sb("slots", [P, 2 * NT], F32, att)
        slots_i = sb("slots_i", [P, 2 * NT], I32, att)
        count_f = sb("count_f", [P, E], F32, att)
        blocks_i = sb("blocks_i", [P, E], I32, att)
        block_f = sb("block_f", [P, E], F32, att)
        first_f = sb("first_f", [P, E], F32, att)
        pad_id = sb("pad_id", [P, MIN_BLOCKS, E], I32, att)

        prep = ExitStack()
        prep_in = sb("prep_in", [P, KC * NB * LC + 3 * KC * D], F32, prep)
        prep_hi = sb("prep_hi", [P, KC * NB * LC + 3 * KC * D], F32R, prep)
        prep_lo = sb("prep_lo", [P, KC * NB * LC + 3 * KC * D], F32R, prep)
        k_f = sb("k_f", [P, KC, NB * LC], F32, prep)
        k_hi = sb("k_hi", [P, KC, NB * LC], F32R, prep)
        k_lo = sb("k_lo", [P, KC, NB * LC], F32R, prep)
        v_f = sb("v_f", [P, NB * 2 * D], F32, prep)
        mask_i = sb("mask_i", [P, NB * LC], I32, prep)
        keep = sb("keep", [P, NB * LC], F32, prep)
        masked = sb("masked", [P, NB * LC], F32, prep)
        bias_cols = sb("bias_cols", [P, 2, KC], F32, prep)
        bq_hi = sb("bq_hi", [P, KC, P], F32R, prep)
        bq_lo = sb("bq_lo", [P, KC, P], F32R, prep)
        bv_row = sb("bv_row", [P, D], F32, prep)
        prep.close()
        sc = sb("sc", [P, NT, LC], F32, att)
        p_hi = [sb(f"p_hi{q}", [CH, 2, TQ * P], F32R, att) for q in range(2)]
        p_lo = [sb(f"p_lo{q}", [CH, 2, TQ * P], F32R, att) for q in range(2)]
        x2 = sb("x2", [P, NT, D], F32, att)
        rows = sb("rows", [P, NT, ROW], F32, att)
        att.close()

        w_hi.append(sb("w_hi1", [P, WCOLS], F32R))
        w_lo.append(sb("w_lo1", [P, WCOLS], F32R))
        block_rows = sb("block_rows", [P, D], F32)
        xt_hi = sb("xt_hi", [P, KC, P], F32R)
        xt_lo = sb("xt_lo", [P, KC, P], F32R)
        u_sb = [sb(f"u_sb{h}", [P, FH], F32) for h in range(2)]
        h_sb = [sb(f"h_sb{h}", [P, FH], F32) for h in range(2)]
        ht_hi = [sb(f"ht_hi{h}", [P, FC // 2, P], F32R) for h in range(2)]
        ht_lo = [sb(f"ht_lo{h}", [P, FC // 2, P], F32R) for h in range(2)]
        weight_token = sb("weight_token", [P, 2], F32)
        y_sb = sb("y_sb", [P, D], F32)

        turned = [ps[:, 4 * q:4 * q + 2, :] for q in range(2)]
        prods = [ps[:, 4 * q + 2:4 * q + 4, :] for q in range(2)]
        logits = prods[0][:, 0, 0:NT * E]
        ranks = prods[1][:, 0, 0:NT * E]
        g_ps = [ps[:, 0, :], ps[:, 1, :]]
        u_ps = [ps[:, 2, :], ps[:, 3, :]]
        ht_ps = [ps[:, 4, :], ps[:, 5, :]]
        xt_ps = ps[:, 6, 0:D]
        y_ps = ps[:, 7, 0:D]

        pool_waited = sem("pool_waited")
        dve_waited = sem("dve_waited")
        sp_waited = sem("sp_waited")
        prep_loaded = sem("prep_loaded")
        small_loaded = sem("small_loaded")
        x_loaded = sem("x_loaded")
        raw_loaded = sem("raw_loaded")
        consts_made = sem("consts_made")
        pool_step = sem("pool_step")
        dve_step = sem("dve_step")
        act_step = sem("act_step")
        prep_split_hi = sem("prep_split_hi")
        prep_split = sem("prep_split")
        wr_split_hi = sem("wr_split_hi")
        k_made = sem("k_made")
        k_masked = sem("k_masked")
        k_split_hi = sem("k_split_hi")
        k_split = sem("k_split")
        v_made = sem("v_made")
        v_biased = sem("v_biased")
        v_split_hi = sem("v_split_hi")
        m_made = sem("m_made")
        m_split_hi = sem("m_split_hi")
        m_split = sem("m_split")
        bqk_made = sem("bqk_made")
        first_split = sem("first_split")
        var_ready = sem("var_ready")
        guess_ready = sem("guess_ready")
        xn_ready = sem("xn_ready")
        x_turned = sem("x_turned")
        xt_split_hi = sem("xt_split_hi")
        xt_split = sem("xt_split")
        scored = sem("scored")
        maxed = sem("maxed")
        exped = sem("exped")
        p_turned = sem("p_turned")
        pt_split_hi = sem("pt_split_hi")
        pt_split = sem("pt_split")
        attended = sem("attended")
        x2_made = sem("x2_made")
        x2_stored = sem("x2_stored")
        xn2_ready = sem("xn2_ready")
        x2_turned = sem("x2_turned")
        x2t_split_hi = sem("x2t_split_hi")
        x2t_split = sem("x2t_split")
        logits_ready = sem("logits_ready")
        below_ready = sem("below_ready")
        second_ready = sem("second_ready")
        route_exped = sem("route_exped")
        picked_ready = sem("picked_ready")
        ranked = sem("ranked")
        slots_ready = sem("slots_ready")
        rows_scattered = sem("rows_scattered")
        counted = sem("counted")
        plan_ready = sem("plan_ready")
        pads_ready = sem("pads_ready")
        pads_stored = sem("pads_stored")
        dummy_stored = sem("dummy_stored")
        block_loaded = sem("block_loaded")
        block_turned = sem("block_turned")
        bt_split_hi = sem("bt_split_hi")
        bt_split = sem("bt_split")
        gu_done = [sem(f"gu_done{h}") for h in range(2)]
        u_copied = [sem(f"u_copied{h}") for h in range(2)]
        h_made = [sem(f"h_made{h}") for h in range(2)]
        h_turned = [sem(f"h_turned{h}") for h in range(2)]
        ht_split_hi = [sem(f"ht_split_hi{h}") for h in range(2)]
        ht_split = [sem(f"ht_split{h}") for h in range(2)]
        w_split_hi = sem("w_split_hi")
        w_split = sem("w_split")
        y_done = sem("y_done")
        y_weighted = sem("y_weighted")
        meta_loaded = sem("meta_loaded")
        y_added = sem("y_added")

        ctx_hi = prep_hi[:, 0:KC * NB * LC].rearrange("p (k n) -> p k n", k=KC)
        ctx_lo = prep_lo[:, 0:KC * NB * LC].rearrange("p (k n) -> p k n", k=KC)

        def small_w(t, n):
            o = KC * NB * LC + n * KC * D
            return t[:, o:o + KC * D].rearrange("p (k n) -> p k n", k=KC)

        x_v = x.rearrange("(b p t) d -> b p (t d)", p=P, t=NT)
        out_v = out[0:T, :].rearrange("(b p t) d -> b p (t d)", p=P, t=NT)
        block = whole.enter_context(nc.Block())

        @block.sync
        def _(sp):
            sp.dma_start(prep_in[:], w_small).then_inc(prep_loaded, 16)
            sp.dma_start(xb[:].rearrange("p t d -> p (t d)"), x_v[0]).then_inc(x_loaded, 16)
            sp.dma_start(mask_i[:], mask.partition_broadcast(P)).then_inc(small_loaded, 16)
            sp.dma_start(bias_cols[:, 0, :], bq).then_inc(small_loaded, 16)
            sp.dma_start(bias_cols[:, 1, :], bk).then_inc(small_loaded, 16)
            sp.dma_start(bv_row[:], bv.partition_broadcast(P)).then_inc(small_loaded, 16)
            sp.dma_start(gate_in[:], gates.partition_broadcast(P)).then_inc(small_loaded, 16)
            sp.dma_start(wr_f[:].rearrange("p k e -> p (k e)"), wr_t).then_inc(small_loaded, 16)
            sp.dma_start(w_raw[:], w_experts[0]).then_inc(raw_loaded, 16)
            sp.wait_ge(pads_ready, 1)
            sp.dma_start(out[T:T + P, :], pads[:, 0, 0:D]).then_inc(dummy_stored, 16)

            with sp.Fori(0, NB) as i:
                sp.wait_ge(x2_made, i * 2 + 2)
                sp.sem_inc(sp_waited)
                sp.dma_start(out_v[bass.ds(i, 1)].squeeze(0), x2[:].rearrange("p t d -> p (t d)")
                             ).then_inc(x2_stored, 16)
                nxt = (i + 1) & (NB - 1)
                sp.dma_start(xb[:].rearrange("p t d -> p (t d)"), x_v[bass.ds(nxt, 1)].squeeze(0)
                             ).then_inc(x_loaded, 16)

            sp.wait_ge(first_split, 1)
            sp.dma_start(w_raw[:], w_experts[1]).then_inc(raw_loaded, 16)

            sp.wait_ge(plan_ready, 1)
            for e in range(E):
                n = sp.value_load(count_row[0:1, e:e + 1], min_val=0, max_val=T)
                at = n + e * REGION
                sp.dma_start(rows_dram[bass.ds(at, PAD), :].rearrange("(p k) c -> p (k c)", p=P),
                             pads[:].rearrange("p k c -> p (k c)")).then_inc(pads_stored, 16)
            sp.wait_ge(pads_stored, 16 * E)
            sp.wait_ge(rows_scattered, 16 * 2 * NT * NB)

            def load_block(row, blk):
                sp.wait_ge(block_turned, blk)
                sp.sem_inc(sp_waited)
                sp.dma_start(block_rows[:], rows_dram[bass.ds(row, P), 0:D]).then_inc(block_loaded, 16)

            load_block(0, 0)
            with sp.Fori(0, E // 2) as pair:
                for odd in range(2):
                    e = pair * 2 + odd
                    n = sp.value_load(last_row[0:1, bass.ds(e, 1)], min_val=MIN_BLOCKS - 1, max_val=T // P - 1)
                    b0 = sp.value_load(first_row[0:1, bass.ds(e, 1)], min_val=0, max_val=T)
                    load_block(e * REGION + P, b0 + 1)
                    load_block(e * REGION + 2 * P, b0 + 2)
                    sp.wait_ge(w_split, e * PIECES + PIECES)
                    sp.sem_inc(sp_waited)
                    sp.dma_start(w_raw[:], w_experts[bass.ds((e + 2) & (E - 1), 1)].squeeze(0)
                                 ).then_inc(raw_loaded, 16)
                    with sp.Fori(3, n + 1) as j:
                        load_block(e * REGION + j * P, b0 + j)
                    load_block(((e + 1) & (E - 1)) * REGION, b0 + n + 1)
            sp.wait_ge(raw_loaded, 16 * (E + 2))
            sp.wait_ge(x_loaded, 16 * (NB + 1))
            sp.wait_ge(x2_stored, 16 * NB)
            sp.wait_ge(dummy_stored, 16)

        @block.gpsimd
        def _(pool):
            step = Steps(pool, pool_step)
            pool.memset(ident[:], 0.0)
            pool.memset(earlier[:], 1.0)
            pool.memset(ones[:], 1.0)
            pool.memset(picked_before[:], 0.0)
            pool.iota(iota_i[:, 0, :], [[-1, E]], base=E, channel_multiplier=0)
            pool.iota(iota_i[:, 1, :], [[REGION, E]], base=0, channel_multiplier=0)
            pool.iota(pad_id[:], [[1, MIN_BLOCKS], [0, E]], base=0, channel_multiplier=MIN_BLOCKS)
            row_words = rows[:, :, D:ROW].bitcast(I32).rearrange("p t (e two) -> p t e two", two=2)[:, :, :, 1]
            step.mark(pool.memset(pads[:], 0.0))
            step.settle()
            pool.affine_select(out=ident[:], in_=ident[:], compare_op=ALU.not_equal, fill=1.0, base=0,
                               pattern=[[-1, P]], channel_multiplier=1)
            pool.affine_select(out=earlier[:], in_=earlier[:], compare_op=ALU.is_gt, fill=0.0, base=0,
                               pattern=[[1, P]], channel_multiplier=-1).then_inc(consts_made, 1)

            pool.wait_ge(raw_loaded, 16)
            for c in range(PIECES):
                cols = slice(c * PIECE, (c + 1) * PIECE)
                step.mark(pool.tensor_scalar(w_hi[0][:, cols], w_raw[:, cols], 1.0, None, ALU.mult))
            step.settle()
            for c in range(PIECES):
                cols = slice(c * PIECE, (c + 1) * PIECE)
                last = pool.tensor_tensor(w_lo[0][:, cols], w_raw[:, cols], w_hi[0][:, cols].bitcast(F32),
                                          ALU.subtract)
            last.then_inc(first_split, 1)

            pool.wait_ge(bqk_made, 1)
            step.mark(pool.iota(row_words, [[1, NT], [0, E]], base=-S, channel_multiplier=NT))
            step.settle()
            with pool.Fori(0, NB) as i:
                step.loop(i, 1)
                pool.wait_ge(rows_scattered, i * (16 * 2 * NT))
                pool.sem_inc(pool_waited)
                step.mark(pool.tensor_scalar(row_words, row_words, float(S), None, ALU.add))
                step.settle()
                pool.wait_ge(slots_ready, i + 1)
                pool.sem_inc(pool_waited)
                for k in range(2):
                    for t in range(NT):
                        pool.indirect_dma_start(
                            rows_dram,
                            bass.IndirectOffsetOnAxis(ap=slots_i[:, k * NT + t:k * NT + t + 1], axis=0),
                            rows[:, t, :], None).then_inc(rows_scattered, 16)
            step.leave(NB)

            pool.wait_ge(plan_ready, 1)
            pool.wait_ge(pads_stored, 16 * E)
            pool.wait_ge(rows_scattered, 16 * 2 * NT * NB)
            pool.wait_ge(x2_stored, 16 * NB)
            pool.wait_ge(dummy_stored, 16)
            with pool.Fori(0, E) as e:
                n = pool.value_load(last_row[0:1, bass.ds(e, 1)], min_val=MIN_BLOCKS - 1, max_val=T // P - 1)
                b0 = pool.value_load(first_row[0:1, bass.ds(e, 1)], min_val=0, max_val=T)
                with pool.Fori(0, n + 1) as j:
                    pool.wait_ge(y_added, (b0 + j) * 16)
                    pool.dma_start(weight_token[:],
                                   rows_dram[bass.ds(e * REGION + j * P, P), bass.ds(e * 2 + D, 2)]
                                   ).then_inc(meta_loaded, 16)
                    pool.wait_ge(meta_loaded, (b0 + j) * 16 + 16)
                    pool.wait_ge(y_weighted, b0 + j + 1)
                    pool.sem_inc(pool_waited)
                    pool.indirect_dma_start(
                        out, bass.IndirectOffsetOnAxis(ap=weight_token[:, 1:2].bitcast(I32), axis=0),
                        y_sb[:], None, compute_op=ALU.add).then_inc(y_added, 16)
            n = pool.value_load(last_row[0:1, E - 1:E], min_val=MIN_BLOCKS - 1, max_val=T // P - 1)
            b0 = pool.value_load(first_row[0:1, E - 1:E], min_val=0, max_val=T)
            pool.wait_ge(y_added, (b0 + n) * 16 + 16)

        @block.scalar
        def _(act):
            step = Steps(act, act_step)
            act.wait_ge(small_loaded, 16 * 6)
            step.mark(act.activation(gate[:], gate_in[:], ACT.Tanh))
            act.copy(wr_hi[:], wr_f[:]).then_inc(wr_split_hi, 1)
            act.wait_ge(prep_loaded, 16)
            act.copy(prep_hi[:], prep_in[:]).then_inc(prep_split_hi, 1)
            act.preload_act_table_set("natural_log_exp_and_others")
            act.wait_ge(k_masked, 1)
            act.copy(k_hi[:], k_f[:]).then_inc(k_split_hi, 1)
            act.wait_ge(v_biased, 1)
            act.copy(v_hi[0:CH, :], v_f[0:CH, :]).then_inc(v_split_hi, 1)
            act.wait_ge(m_made, 1)
            for m in range(KC):
                last = act.copy(m_hi[:, m * NB * LC:(m + 1) * NB * LC].rearrange("p (h n) -> p h n", h=2),
                                ps[:, 2 * m:2 * m + 2, 0:2 * LC])
            last.then_inc(m_split_hi, 1)

            def guess_rstd(n):
                act.wait_ge(var_ready, n)
                step.mark(act.activation(ln_l[:], ln_v[:], ACT.Ln))
                step.settle()
                act.activation(ln_y[:], ln_l[:], ACT.Exp, scale=-0.5).then_inc(guess_ready, 1)

            with act.Fori(0, NB) as i:
                step.loop(i, 2)
                guess_rstd(i * 2 + 1)
                for q in range(2):
                    act.wait_ge(x_turned, i * 2 + q + 1)
                    act.copy(t_hi[q][:], turned[q]).then_inc(xt_split_hi, 1)
                for q in range(2):
                    act.wait_ge(maxed, i * 2 + q + 1)
                    for t in range(q * TQ, (q + 1) * TQ):
                        last = act.activation(sc[:, t, :], sc[:, t, :], ACT.Exp, bias=neg_max[:, t:t + 1],
                                              scale=-1.0, accum_out=exp_sum[:, t:t + 1])
                    last.then_inc(exped, 1)
                for q in range(2):
                    act.wait_ge(p_turned, i * 2 + q + 1)
                    act.copy(p_hi[q][:], turned[q][0:CH]).then_inc(pt_split_hi, 1)
                guess_rstd(i * 2 + 2)
                for q in range(2):
                    act.wait_ge(x2_turned, i * 2 + q + 1)
                    act.copy(t_hi[q][:], turned[q]).then_inc(x2t_split_hi, 1)
                act.wait_ge(below_ready, i + 1)
                act.activation(ex[:], below[:], ACT.Exp)
                act.wait_ge(second_ready, i + 1)
                act.activation(ratio[:], second[:], ACT.Exp).then_inc(route_exped, 1)
            step.leave(NB)

            act.wait_ge(plan_ready, 1)

            def piece(e, odd, c):
                cols = slice(c * PIECE, (c + 1) * PIECE)
                act.copy(w_hi[1 - odd][:, cols], w_raw[:, cols]).then_inc(w_split_hi, 1)

            def copy_u(h, blk):
                act.wait_ge(gu_done[h], blk + 1)
                act.copy(u_sb[h][:], u_ps[h]).then_inc(u_copied[h], 1)

            def split_h(h, blk):
                act.wait_ge(h_turned[h], blk + 1)
                act.copy(ht_hi[h][:].rearrange("p c t -> p (c t)"), ht_ps[h]).then_inc(ht_split_hi[h], 1)

            def split_x(blk):
                act.wait_ge(block_turned, blk + 1)
                act.copy(xt_hi[:].rearrange("p k t -> p (k t)"), xt_ps).then_inc(bt_split_hi, 1)

            split_x(0)
            with act.Fori(0, E // 2) as pair:
                for odd in range(2):
                    e = pair * 2 + odd
                    n = act.value_load(last_row[0:1, bass.ds(e, 1)], min_val=MIN_BLOCKS - 1, max_val=T // P - 1)
                    b0 = act.value_load(first_row[0:1, bass.ds(e, 1)], min_val=0, max_val=T)
                    copy_u(0, b0)
                    act.wait_ge(raw_loaded, e * 16 + 32)
                    act.wait_ge(y_done, b0)
                    piece(e, odd, 0)
                    piece(e, odd, 1)
                    copy_u(1, b0)
                    split_x(b0 + 1)
                    split_h(0, b0)
                    piece(e, odd, 2)
                    piece(e, odd, 3)
                    copy_u(0, b0 + 1)
                    split_h(1, b0)
                    piece(e, odd, 4)
                    copy_u(1, b0 + 1)
                    split_x(b0 + 2)
                    split_h(0, b0 + 1)
                    piece(e, odd, 5)
                    with act.Fori(1, n) as j:
                        copy_u(0, b0 + j + 1)
                        split_h(1, b0 + j)
                        copy_u(1, b0 + j + 1)
                        split_x(b0 + j + 2)
                        split_h(0, b0 + j + 1)
                    split_h(1, b0 + n)

        @block.vector
        def _(dve):
            step = Steps(dve, dve_step)

            dve.wait_ge(small_loaded, 16 * 6)
            dve.wait_ge(consts_made, 1)
            dve.tensor_scalar(keep[:], mask_i[:], 0.0, None, ALU.not_equal)
            dve.tensor_copy(bq_hi[:], bias_cols[:, 0, :].unsqueeze(2).broadcast_to([P, KC, P]))
            dve.tensor_copy(falling[:], iota_i[:, 0, :])
            dve.tensor_copy(region0[:], iota_i[:, 1, :])
            dve.wait_ge(wr_split_hi, 1)
            dve.tensor_tensor(wr_lo[:], wr_f[:], wr_hi[:].bitcast(F32), ALU.subtract)
            step.mark(dve.tensor_scalar(pad_id[:], pad_id[:], P - 1, None, ALU.bitwise_and))
            step.settle()
            pad_words = pads[:, :, D:ROW].bitcast(I32).rearrange("p k (e two) -> p k e two", two=2)[:, :, :, 1]
            dve.tensor_scalar(pad_words, pad_id[:], float(T), None, ALU.add).then_inc(pads_ready, 1)
            dve.tensor_scalar(masked[:], keep[:], -MASKED, MASKED, ALU.mult, ALU.add)
            dve.tensor_tensor(bq_lo[:], bias_cols[:, 0, :].unsqueeze(2).broadcast_to([P, KC, P]),
                              bq_hi[:].bitcast(F32), ALU.subtract)
            dve.wait_ge(prep_split_hi, 1)
            dve.tensor_tensor(prep_lo[:], prep_in[:], prep_hi[:].bitcast(F32), ALU.subtract
                              ).then_inc(prep_split, 1)
            dve.wait_ge(k_made, 1)
            for m in range(KC):
                for h in range(2):
                    cols = slice(h * 2 * LC, (h + 1) * 2 * LC)
                    last = dve.scalar_tensor_tensor(k_f[:, m, cols], ps[:, 2 * m + h, 0:2 * LC],
                                                    bias_cols[:, 1, m:m + 1], keep[:, cols], ALU.add, ALU.mult)
            last.then_inc(k_masked, 1)
            dve.wait_ge(k_split_hi, 1)
            dve.tensor_tensor(k_lo[:], k_f[:], k_hi[:].bitcast(F32), ALU.subtract).then_inc(k_split, 1)
            dve.wait_ge(v_made, 1)
            dve.tensor_tensor(v_f[0:CH, :].rearrange("p (n d) -> p n d", d=D),
                              ps[0:CH, 4:8, :].rearrange("p k (n d) -> p (k n) d", d=D),
                              bv_row[0:CH, :].unsqueeze(1).broadcast_to([CH, 2 * NB, D]), ALU.add
                              ).then_inc(v_biased, 1)
            dve.wait_ge(v_split_hi, 1)
            dve.tensor_tensor(v_lo[0:CH, :], v_f[0:CH, :], v_hi[0:CH, :].bitcast(F32), ALU.subtract)
            dve.wait_ge(m_split_hi, 1)
            for m in range(KC):
                cols = slice(m * NB * LC, (m + 1) * NB * LC)
                last = dve.tensor_tensor(m_lo[:, cols].rearrange("p (h n) -> p h n", h=2),
                                         ps[:, 2 * m:2 * m + 2, 0:2 * LC],
                                         m_hi[:, cols].bitcast(F32).rearrange("p (h n) -> p h n", h=2), ALU.subtract)
            dve.wait_ge(bqk_made, 1)
            dve.tensor_tensor(bias_all[:].rearrange("p (h n) -> p h n", h=2), ps[:, 4:6, 0:2 * LC],
                              masked[:].rearrange("p (h n) -> p h n", h=2), ALU.add).then_inc(m_split, 1)
            dve.wait_ge(m_split, 1)
            step.mark(dve.memset(picked_now[:], 0.0))

            def newton(n):
                dve.wait_ge(guess_ready, n)
                step.mark(dve.scalar_tensor_tensor(ln_a[:], ln_v[:], -0.5, ln_y[:], ALU.mult, ALU.mult))
                step.settle()
                step.mark(dve.tensor_tensor(ln_b[:], ln_a[:], ln_y[:], ALU.mult))
                step.settle()
                step.mark(dve.scalar_tensor_tensor(rstd[:], ln_b[:], 1.5, ln_y[:], ALU.add, ALU.mult))
                step.settle()

            with dve.Fori(0, NB) as i:
                step.loop(i, DVE_STEPS)
                step.mark(dve.tensor_copy(bias_now[:], bias_all[:, bass.ds(i * LC, LC)]))
                dve.wait_ge(x_loaded, i * 16 + 16)
                for t in range(NT):
                    step.mark(dve.bn_stats(stats[:, t, :], xb[:, t, :]))
                step.settle()
                dve.sem_inc(dve_waited)
                for t in range(NT):
                    step.mark(dve.bn_aggr(moments[:, t, :], stats[:, t, :]))
                step.settle()
                dve.tensor_scalar(ln_v[:], moments[:, :, 1], LN_EPS, None, ALU.add).then_inc(var_ready, 1)
                newton(i * 2 + 1)
                for q in range(2):
                    for t in range(q * TQ, (q + 1) * TQ):
                        last = dve.tensor_scalar(xn[:, t, :], xb[:, t, :], moments[:, t, 0:1], rstd[:, t:t + 1],
                                                 ALU.subtract, ALU.mult)
                    last.then_inc(xn_ready, 1)
                for q in range(2):
                    dve.wait_ge(xt_split_hi, i * 2 + q + 1)
                    dve.tensor_tensor(t_lo[q][:], turned[q], t_hi[q][:].bitcast(F32), ALU.subtract
                                      ).then_inc(xt_split, 1)
                for q in range(2):
                    dve.wait_ge(scored, i * 2 + q + 1)
                    dve.sem_inc(dve_waited)
                    for t in range(TQ):
                        last = dve.tensor_tensor_reduce(
                            out=sc[:, q * TQ + t, :], in0=prods[q][:, t // 2, (t % 2) * D:(t % 2) * D + LC],
                            in1=bias_now[:], scale=-float(D) ** -0.5, scalar=3e38, op0=ALU.add, op1=ALU.min,
                            accum_out=neg_max[:, q * TQ + t:q * TQ + t + 1])
                    last.then_inc(maxed, 1)
                for q in range(2):
                    dve.wait_ge(pt_split_hi, i * 2 + q + 1)
                    dve.tensor_tensor(p_lo[q][:], turned[q][0:CH], p_hi[q][:].bitcast(F32), ALU.subtract
                                      ).then_inc(pt_split, 1)
                step.mark(dve.reciprocal(exp_inv[:], exp_sum[:]))
                step.settle()
                step.mark(dve.tensor_scalar(att_scale[:], exp_inv[:], gate[:, 0:1], None, ALU.mult))
                step.settle()
                dve.wait_ge(x2_stored, i * 16)
                for q in range(2):
                    dve.wait_ge(attended, i * 2 + q + 1)
                    for t in range(q * TQ, (q + 1) * TQ):
                        last = dve.scalar_tensor_tensor(
                            x2[:, t, :], prods[q][:, (t % TQ) // 2, (t % 2) * D:(t % 2 + 1) * D],
                            att_scale[:, t:t + 1], xb[:, t, :], ALU.mult, ALU.add)
                    last.then_inc(x2_made, 1)
                dve.wait_ge(x2_made, i * 2 + 2)
                for t in range(NT):
                    step.mark(dve.bn_stats(stats[:, t, :], x2[:, t, :]))
                step.settle()
                dve.sem_inc(dve_waited)
                for t in range(NT):
                    step.mark(dve.bn_aggr(moments[:, t, :], stats[:, t, :]))
                step.settle()
                dve.tensor_scalar(ln_v[:], moments[:, :, 1], LN_EPS, None, ALU.add).then_inc(var_ready, 1)
                newton(i * 2 + 2)
                dve.wait_ge(rows_scattered, i * (16 * 2 * NT))
                for q in range(2):
                    for t in range(q * TQ, (q + 1) * TQ):
                        last = dve.tensor_scalar(rows[:, t, 0:D], x2[:, t, :], moments[:, t, 0:1],
                                                 rstd[:, t:t + 1], ALU.subtract, ALU.mult)
                    last.then_inc(xn2_ready, 1)
                for q in range(2):
                    dve.wait_ge(x2t_split_hi, i * 2 + q + 1)
                    dve.tensor_tensor(t_lo[q][:], turned[q], t_hi[q][:].bitcast(F32), ALU.subtract
                                      ).then_inc(x2t_split, 1)
                lg = logits.rearrange("p (t e) -> p t e", e=E)
                fall = falling[:].unsqueeze(1).broadcast_to([P, NT, E])
                dve.wait_ge(logits_ready, i + 1)
                step.mark(dve.tensor_reduce(best[:], lg, AX.X, ALU.max))
                step.settle()
                dve.tensor_tensor(below[:], lg, best[:].unsqueeze(2).broadcast_to([P, NT, E]), ALU.subtract
                                  ).then_inc(below_ready, 1)
                dve.wait_ge(below_ready, i + 1)

                def choose(k, n):
                    step.mark(dve.tensor_reduce(best[:], cand[:], AX.X, ALU.max))
                    step.settle()
                    step.mark(dve.tensor_tensor(chosen[:, k], cand[:],
                                                best[:].unsqueeze(2).broadcast_to([P, NT, E]), ALU.is_equal))
                    step.settle()

                step.mark(dve.tensor_scalar(cand[:], below[:], 0.0, None, ALU.is_ge))
                step.settle()
                step.mark(dve.tensor_tensor(cand[:], cand[:], fall, ALU.mult))
                step.settle()
                choose(0, i)
                step.mark(dve.scalar_tensor_tensor(place[:].rearrange("p t e -> p (t e)"),
                                                   chosen[:, 0].rearrange("p t e -> p (t e)"), BELOW,
                                                   below[:].rearrange("p t e -> p (t e)"), ALU.mult, ALU.add))
                step.settle()
                dve.tensor_reduce(second[:], place[:], AX.X, ALU.max).then_inc(second_ready, 1)
                dve.wait_ge(second_ready, i + 1)
                step.mark(dve.tensor_tensor(cand[:], place[:], second[:].unsqueeze(2).broadcast_to([P, NT, E]),
                                            ALU.is_ge))
                step.settle()
                step.mark(dve.tensor_tensor(cand[:], cand[:], fall, ALU.mult))
                step.settle()
                choose(1, i)
                dve.tensor_tensor(picked[:], chosen[:, 0], chosen[:, 1], ALU.add).then_inc(picked_ready, 1)
                dve.wait_ge(route_exped, i + 1)
                step.mark(dve.tensor_reduce(e_sum[:], ex[:], AX.X, ALU.add))
                step.settle()
                step.mark(dve.scalar_tensor_tensor(den[:], e_sum[:], K_EPS, ratio[:], ALU.mult, ALU.add))
                step.settle()
                step.mark(dve.tensor_scalar(den[:], den[:], 1.0, None, ALU.add))
                step.settle()
                step.mark(dve.reciprocal(w_first[:], den[:]))
                step.settle()
                step.mark(dve.tensor_scalar(w_first[:], w_first[:], gate[:, 1:2], None, ALU.mult))
                step.settle()
                step.mark(dve.tensor_tensor(w_second[:], w_first[:], ratio[:], ALU.mult))
                step.settle()
                dve.tensor_tensor(cand[:], chosen[:, 0], w_first[:].unsqueeze(2).broadcast_to([P, NT, E]), ALU.mult)
                step.mark(dve.tensor_tensor(place[:], chosen[:, 1],
                                            w_second[:].unsqueeze(2).broadcast_to([P, NT, E]), ALU.mult))
                step.settle()
                row_weights = rows[:, :, D:ROW].rearrange("p t (e two) -> p t e two", two=2)[:, :, :, 0]
                step.mark(dve.tensor_tensor(row_weights, cand[:], place[:], ALU.add))
                step.settle()
                dve.wait_ge(ranked, i + 1)
                step.mark(dve.tensor_tensor(place[:], ranks.rearrange("p (t e) -> p t e", e=E),
                                            region0[:].unsqueeze(1).broadcast_to([P, NT, E]), ALU.add))
                step.mark(dve.tensor_reduce(picked_now[:], picked[:].rearrange("p t e -> p e t"), AX.X, ALU.add))
                step.settle()
                step.mark(dve.tensor_tensor(slot_of[:, 0], chosen[:, 0], place[:], ALU.mult))
                step.mark(dve.tensor_tensor(slot_of[:, 1], chosen[:, 1], place[:], ALU.mult))
                step.mark(dve.tensor_tensor(picked_before[:], picked_before[:], picked_now[:], ALU.add))
                step.settle()
                step.mark(dve.tensor_reduce(slots[:], slot_of[:].rearrange("p k t e -> p (k t) e"), AX.X, ALU.add))
                step.settle()
                dve.tensor_copy(slots_i[:], slots[:]).then_inc(slots_ready, 1)
            step.leave(NB)

            dve.wait_ge(counted, 1)
            dve.tensor_copy(count_row[:], ranks[:, 0:E])
            step.mark(dve.tensor_scalar(blocks_i[:], ranks[:, 0:E], float(P - 1), None, ALU.add))
            step.settle()
            step.mark(dve.tensor_scalar(blocks_i[:], blocks_i[:], P.bit_length() - 1, None,
                                        ALU.logical_shift_right))
            step.settle()
            step.mark(dve.tensor_scalar(block_f[:], blocks_i[:], float(MIN_BLOCKS), None, ALU.max))
            step.settle()
            step.mark(dve.tensor_scalar(last_row[:], block_f[:], -1.0, None, ALU.add))
            step.mark(dve.memset(first_f[:], 0.0))
            step.settle()
            for e in range(1, E):
                step.mark(dve.tensor_tensor(first_f[:, e:e + 1], first_f[:, e - 1:e], block_f[:, e - 1:e], ALU.add))
                step.settle()
            dve.tensor_copy(first_row[:], first_f[:]).then_inc(plan_ready, 1)
            dve.wait_ge(plan_ready, 1)

            def piece(e, odd, c):
                cols = slice(c * PIECE, (c + 1) * PIECE)
                dve.wait_ge(w_split_hi, e * PIECES + (c + 1))
                dve.tensor_tensor(w_lo[1 - odd][:, cols], w_raw[:, cols], w_hi[1 - odd][:, cols].bitcast(F32),
                                  ALU.subtract).then_inc(w_split, 1)

            def make_h(h, blk):
                dve.wait_ge(u_copied[h], blk + 1)
                dve.scalar_tensor_tensor(h_sb[h][:], g_ps[h], 0.0, u_sb[h][:], ALU.max, ALU.mult
                                         ).then_inc(h_made[h], 1)

            def split_h(h, blk):
                dve.wait_ge(ht_split_hi[h], blk + 1)
                dve.tensor_tensor(ht_lo[h][:].rearrange("p c t -> p (c t)"), ht_ps[h],
                                  ht_hi[h][:].bitcast(F32).rearrange("p c t -> p (c t)"), ALU.subtract
                                  ).then_inc(ht_split[h], 1)

            def split_x(blk):
                dve.wait_ge(bt_split_hi, blk + 1)
                dve.tensor_tensor(xt_lo[:].rearrange("p k t -> p (k t)"), xt_ps,
                                  xt_hi[:].bitcast(F32).rearrange("p k t -> p (k t)"), ALU.subtract
                                  ).then_inc(bt_split, 1)

            def weigh_y(blk):
                dve.wait_ge(y_done, blk + 1)
                dve.wait_ge(meta_loaded, blk * 16 + 16)
                dve.wait_ge(y_added, blk * 16)
                dve.tensor_scalar(y_sb[:], y_ps, weight_token[:, 0:1], None, ALU.mult).then_inc(y_weighted, 1)

            split_x(0)
            with dve.Fori(0, E // 2) as pair:
                for odd in range(2):
                    e = pair * 2 + odd
                    n = dve.value_load(last_row[0:1, bass.ds(e, 1)], min_val=MIN_BLOCKS - 1, max_val=T // P - 1)
                    b0 = dve.value_load(first_row[0:1, bass.ds(e, 1)], min_val=0, max_val=T)
                    make_h(0, b0)
                    piece(e, odd, 0)
                    make_h(1, b0)
                    split_x(b0 + 1)
                    split_h(0, b0)
                    piece(e, odd, 1)
                    piece(e, odd, 2)
                    make_h(0, b0 + 1)
                    split_h(1, b0)
                    piece(e, odd, 3)
                    piece(e, odd, 4)
                    make_h(1, b0 + 1)
                    split_x(b0 + 2)
                    split_h(0, b0 + 1)
                    weigh_y(b0)
                    piece(e, odd, 5)
                    with dve.Fori(1, n) as j:
                        make_h(0, b0 + j + 1)
                        split_h(1, b0 + j)
                        make_h(1, b0 + j + 1)
                        split_x(b0 + j + 2)
                        split_h(0, b0 + j + 1)
                        weigh_y(b0 + j)
                    split_h(1, b0 + n)
                    weigh_y(b0 + n)

        @block.tensor
        def _(pe):
            def product(o, lhs, rhs, first, last):
                pe.matmul(o, lhs[0], rhs[0], start=first, stop=False)
                pe.matmul(o, lhs[0], rhs[1], start=False, stop=False)
                return pe.matmul(o, lhs[1], rhs[0], start=False, stop=last)

            wk = [small_w(t, 0) for t in (prep_hi, prep_lo)]
            wv = [small_w(t, 1) for t in (prep_hi, prep_lo)]
            wq = [small_w(t, 2) for t in (prep_hi, prep_lo)]
            ctx = [ctx_hi, ctx_lo]
            kk = [k_hi, k_lo]
            pe.wait_ge(prep_split, 1)
            for m in range(KC):
                for h in range(2):
                    for k in range(KC):
                        last = product(ps[:, 2 * m + h, 0:2 * LC], [w[:, k, m * P:(m + 1) * P] for w in wk],
                                       [c[:, k, h * 2 * LC:(h + 1) * 2 * LC] for c in ctx], k == 0, k == KC - 1)
            last.then_inc(k_made, 1)
            for n in range(2 * NB):
                for k in range(KC):
                    last = product(ps[0:CH, 4 + n // 2, (n % 2) * D:(n % 2 + 1) * D],
                                   [c[:, k, n * CH:(n + 1) * CH] for c in ctx], [w[:, k, :] for w in wv],
                                   k == 0, k == KC - 1)
            last.then_inc(v_made, 1)
            pe.wait_ge(k_split, 1)
            for m in range(KC):
                for h in range(2):
                    for k in range(KC):
                        last = product(ps[:, 2 * m + h, 0:2 * LC], [w[:, k, m * P:(m + 1) * P] for w in wq],
                                       [t[:, k, h * 2 * LC:(h + 1) * 2 * LC] for t in kk], k == 0, k == KC - 1)
            last.then_inc(m_made, 1)
            pe.wait_ge(v_biased, 1)
            for h in range(2):
                for k in range(KC):
                    last = product(ps[:, 4 + h, 0:2 * LC], [t[:, k, :] for t in (bq_hi, bq_lo)],
                                   [t[:, k, h * 2 * LC:(h + 1) * 2 * LC] for t in kk], k == 0, k == KC - 1)
            last.then_inc(bqk_made, 1)
            pe.wait_ge(m_split, 1)
            pe.wait_ge(consts_made, 1)

            tt = [[t_hi[q], t_lo[q]] for q in range(2)]

            def turn(q, tile):
                for k in range(KC):
                    for t in range(TQ):
                        last = pe.transpose(turned[q][:, k, t * P:(t + 1) * P], tile(q * TQ + t, k), ident[:])
                return last

            with pe.Fori(0, NB) as i:
                for q in range(2):
                    pe.wait_ge(xn_ready, i * 2 + q + 1)
                    turn(q, lambda t, k: xn[:, t, k * P:(k + 1) * P]).then_inc(x_turned, 1)
                pe.wait_ge(slots_ready, i)
                for q in range(2):
                    pe.wait_ge(xt_split, i * 2 + q + 1)
                    for t in range(TQ):
                        for k in range(KC):
                            last = product(prods[q][:, t // 2, (t % 2) * D:(t % 2) * D + LC],
                                           [a[:, k, t * P:(t + 1) * P] for a in tt[q]],
                                           [m[:, bass.ds(i * LC + k * NB * LC, LC)] for m in (m_hi, m_lo)],
                                           k == 0, k == KC - 1)
                    last.then_inc(scored, 1)
                for q in range(2):
                    pe.wait_ge(exped, i * 2 + q + 1)
                    for c in range(2):
                        for t in range(TQ):
                            last = pe.transpose(turned[q][0:CH, c, t * P:(t + 1) * P],
                                                sc[:, q * TQ + t, c * CH:(c + 1) * CH], ident[:])
                    last.then_inc(p_turned, 1)
                for q in range(2):
                    pe.wait_ge(pt_split, i * 2 + q + 1)
                    for t in range(TQ):
                        for c in range(2):
                            last = product(prods[q][:, t // 2, (t % 2) * D:(t % 2 + 1) * D],
                                           [a[:, c, t * P:(t + 1) * P] for a in (p_hi[q], p_lo[q])],
                                           [v[0:CH, bass.ds(i * (2 * D) + c * D, D)] for v in (v_hi, v_lo)],
                                           c == 0, c == 1)
                    last.then_inc(attended, 1)
                for q in range(2):
                    pe.wait_ge(xn2_ready, i * 2 + q + 1)
                    turn(q, lambda t, k: rows[:, t, k * P:(k + 1) * P]).then_inc(x2_turned, 1)
                for q in range(2):
                    pe.wait_ge(x2t_split, i * 2 + q + 1)
                    for t in range(TQ):
                        for k in range(KC):
                            o = (q * TQ + t) * E
                            last = product(logits[:, o:o + E], [a[:, k, t * P:(t + 1) * P] for a in tt[q]],
                                           [w[:, k, :] for w in (wr_hi, wr_lo)], k == 0, k == KC - 1)
                last.then_inc(logits_ready, 1)
                pe.wait_ge(picked_ready, i + 1)
                flat = picked[:].rearrange("p t e -> p (t e)")
                pe.matmul(ranks, earlier[:], flat, start=True, stop=False)
                pe.matmul(ranks.rearrange("p (t e) -> p t e", e=E), ones[:],
                          picked_before[:].unsqueeze(1).broadcast_to([P, NT, E]), start=False, stop=False)
                for back in range(1, NT):
                    last = pe.matmul(ranks[:, back * E:], ones[:], flat[:, 0:(NT - back) * E], start=False,
                                     stop=(back == NT - 1))
                last.then_inc(ranked, 1)

            pe.wait_ge(slots_ready, NB)
            pe.matmul(ranks[:, 0:E], ones[:], picked_before[:], start=True, stop=True).then_inc(counted, 1)

            def w_g(odd, k, h):
                o = k * F + h * FH
                return [w[odd][:, o:o + FH] for w in (w_hi, w_lo)]

            def w_u(odd, k, h):
                o = KC * F + k * F + h * FH
                return [w[odd][:, o:o + FH] for w in (w_hi, w_lo)]

            def w_d(odd, c):
                o = 2 * KC * F + c * D
                return [w[odd][:, o:o + D] for w in (w_hi, w_lo)]

            def gate_up(odd, h, blk):
                pe.wait_ge(h_made[h], blk)
                if h == 0:
                    pe.wait_ge(bt_split, blk + 1)
                for k in range(KC):
                    g, u = w_g(odd, k, h), w_u(odd, k, h)
                    first, last = k == 0, k == KC - 1
                    hi, lo = xt_hi[:, k, :], xt_lo[:, k, :]
                    pe.matmul(g_ps[h], hi, g[0], start=first, stop=False)
                    pe.matmul(g_ps[h], hi, g[1], start=False, stop=False)
                    pe.matmul(u_ps[h], hi, u[0], start=first, stop=False)
                    pe.matmul(u_ps[h], hi, u[1], start=False, stop=False)
                    pe.matmul(g_ps[h], lo, g[0], start=False, stop=last)
                    mm = pe.matmul(u_ps[h], lo, u[0], start=False, stop=last)
                mm.then_inc(gu_done[h], 1)

            def turn_h(h, blk):
                pe.wait_ge(h_made[h], blk + 1)
                pe.wait_ge(ht_split[h], blk)
                for c in range(FC // 2):
                    mm = pe.transpose(ht_ps[h][:, c * P:(c + 1) * P], h_sb[h][:, c * P:(c + 1) * P], ident[:])
                mm.then_inc(h_turned[h], 1)

            def turn_x(blk):
                pe.wait_ge(block_loaded, blk * 16 + 16)
                pe.wait_ge(bt_split, blk)
                for k in range(KC):
                    mm = pe.transpose(xt_ps[:, k * P:(k + 1) * P], block_rows[:, k * P:(k + 1) * P], ident[:])
                mm.then_inc(block_turned, 1)

            def down(odd, h, blk):
                pe.wait_ge(ht_split[h], blk + 1)
                if h == 0:
                    pe.wait_ge(y_weighted, blk)
                for c in range(FC // 2):
                    mm = product(y_ps, [t[h][:, c, :] for t in (ht_hi, ht_lo)], w_d(odd, h * (FC // 2) + c),
                                 h == 0 and c == 0, h == 1 and c == FC // 2 - 1)
                if h == 1:
                    mm.then_inc(y_done, 1)

            def inner_block(odd, blk):
                gate_up(odd, 0, blk + 1)
                turn_h(1, blk)
                turn_x(blk + 2)
                down(odd, 0, blk)
                gate_up(odd, 1, blk + 1)
                down(odd, 1, blk)
                turn_h(0, blk + 1)

            pe.wait_ge(plan_ready, 1)
            pe.wait_ge(first_split, 1)
            turn_x(0)
            with pe.Fori(0, E // 2) as pair:
                for odd in range(2):
                    e = pair * 2 + odd
                    n = pe.value_load(last_row[0:1, bass.ds(e, 1)], min_val=MIN_BLOCKS - 1, max_val=T // P - 1)
                    b0 = pe.value_load(first_row[0:1, bass.ds(e, 1)], min_val=0, max_val=T)
                    pe.wait_ge(w_split, e * PIECES)
                    gate_up(odd, 0, b0)
                    turn_x(b0 + 1)
                    gate_up(odd, 1, b0)
                    turn_h(0, b0)
                    inner_block(odd, b0)
                    with pe.Fori(1, n) as j:
                        inner_block(odd, b0 + j)
                    turn_h(1, b0 + n)
                    down(odd, 0, b0 + n)
                    down(odd, 1, b0 + n)


DVE_STEPS = 65

_INS = ['x', 'ctx_t', 'w_small', 'mask', 'bq', 'bk', 'bv', 'gates', 'wr_t', 'w_experts']


def kernel(x, ctx_1024, mask_BxS2_ik0, g_xattn, g_ffn, L0_xattn_Wq, L0_xattn_bq, L0_xattn_Wk, L0_xattn_bk,
           L0_xattn_Wv, L0_xattn_bv, L0_ffn_Wr, L0_ffn_Wg, L0_ffn_Wu, L0_ffn_Wd):
    import numpy as np
    import concourse.bacc as bacc
    from concourse.bass_utils import run_bass_kernel_spmd

    def by_partition(a):
        a = np.asarray(a)
        return a.reshape(a.shape[0] // P, P, -1).transpose(1, 0, 2)

    def chunks(a):
        return by_partition(a).reshape(P, -1)

    ctx_t = np.asarray(ctx_1024).transpose(2, 0, 1).reshape(D, NB * LC)
    small = [chunks(ctx_t), chunks(L0_xattn_Wk), chunks(L0_xattn_Wv), chunks(np.asarray(L0_xattn_Wq).T)]
    experts = np.empty((E, P, WCOLS), np.float32)
    for e in range(E):
        experts[e] = np.concatenate([chunks(np.asarray(L0_ffn_Wg)[e].T), chunks(np.asarray(L0_ffn_Wu)[e].T),
                                     chunks(np.asarray(L0_ffn_Wd)[e].T)], axis=1)
    arrays = {
        'x': np.asarray(x).reshape(T, D),
        'w_small': np.concatenate(small, axis=1),
        'mask': np.asarray(mask_BxS2_ik0).reshape(NB * LC),
        'bq': np.asarray(L0_xattn_bq).reshape(KC, P).T,
        'bk': np.asarray(L0_xattn_bk).reshape(KC, P).T,
        'bv': np.asarray(L0_xattn_bv),
        'gates': np.concatenate([np.asarray(g_xattn), np.asarray(g_ffn)]),
        'wr_t': chunks(np.asarray(L0_ffn_Wr).T),
        'w_experts': experts,
    }
    nc = bacc.Bacc("TRN2", target_bir_lowering=False, num_devices=1)
    arrays = {f"in_{k}": np.ascontiguousarray(v) for k, v in arrays.items()}
    aps = {k[3:]: nc.dram_tensor(k, v.shape, mybir.dt.from_np(v.dtype), kind="ExternalInput").ap()
           for k, v in arrays.items()}
    out = nc.dram_tensor("out_padded", (T + P, D), F32, kind="ExternalOutput").ap()
    build(nc, ctx_t=None, out=out, **aps)
    r = run_bass_kernel_spmd(nc, [arrays], core_ids=[0])
    return r.results[0]["out_padded"][0:T].reshape(NB, S, D)
```

```python
from contextlib import ExitStack

import concourse.bass as bass
from concourse import mybir

ALU = mybir.AluOpType
ACT = mybir.ActivationFunctionType
AX = mybir.AxisListType
F32 = mybir.dt.float32
F32R = mybir.dt.float32r
BF16 = mybir.dt.bfloat16
I32 = mybir.dt.int32

P = 128
NB, S, D = 4, 1024, 256
T = NB * S
LC = 154
CH = LC // 2
KC = D // P
NT = S // P
TQ = NT // 2
E, F = 8, 1024
FC = F // P
FH = F // 2
WCOLS = 2 * KC * F + FC * D
PIECE = 1024
PIECES = WCOLS // PIECE
MIN_BLOCKS = 4
PAD = MIN_BLOCKS * P
REGION = T + PAD
ROW = D + 2 * E
LN_EPS = 1e-5
K_EPS = 2.0 ** -23
SCATTERED = 16 * 2 * TQ
FREE = 1
MASKED = -1e9 * 16.0
BELOW = -1e30


class Steps:

    def __init__(self, engine, sem):
        self.engine, self.sem, self.base, self.n = engine, sem, 0, 0

    def mark(self, ins):
        ins.then_inc(self.sem, 1)
        self.n += 1

    def settle(self):
        self.engine.wait_ge(self.sem, self.base + self.n)

    def loop(self, i, per):
        self.base, self.per, self.entry = self.n + i * per, per, self.n
        self.n = 0

    def leave(self, turns):
        assert self.n == self.per, (self.n, self.per)
        self.base, self.n = 0, self.entry + turns * self.per


def build(nc, x, ctx_t, w_small, mask, bq, bk, bv, gates, wr_t, w_experts, out):
    rows_dram = nc.dram_tensor("rows_by_expert", [E * REGION, ROW], F32).ap()

    with ExitStack() as whole:
        def sb(name, shape, dt, stack=whole):
            return stack.enter_context(nc.sbuf_tensor(name, shape, dt))

        def sem(name):
            return whole.enter_context(nc.semaphore(name))

        ps = whole.enter_context(nc.psum_tensor("ps", [P, 8, 512], F32))

        w_raw = sb("w_raw", [P, WCOLS], F32)
        w_hi = [sb("w_hi0", [P, WCOLS], F32R)]
        w_lo = [sb("w_lo0", [P, WCOLS], F32R)]
        ident = sb("ident", [P, P], F32)
        earlier = sb("earlier", [P, P], BF16)
        ones = sb("ones", [P, P], BF16)
        gate = sb("gate", [P, 2], F32)
        count_row = sb("count_row", [P, E], I32)
        last_row = sb("last_row", [P, E], I32)
        first_row = sb("first_row", [P, E], I32)
        pads = sb("pads", [P, MIN_BLOCKS, ROW], F32)

        att = ExitStack()
        x_ln = sb("x_ln", [P, NT, D], F32, att)
        t_hi = [sb(f"t_hi{q}", [P, KC, TQ * P], F32R, att) for q in range(2)]
        t_lo = [sb(f"t_lo{q}", [P, KC, TQ * P], F32R, att) for q in range(2)]
        m_hi = sb("m_hi", [P, KC * NB * LC], F32R, att)
        m_lo = sb("m_lo", [P, KC * NB * LC], F32R, att)
        v_hi = sb("v_hi", [P, NB * 2 * D], F32R, att)
        v_lo = sb("v_lo", [P, NB * 2 * D], F32R, att)
        wr_f = sb("wr_f", [P, KC, E], F32, att)
        wr_pair = sb("wr_pair", [P, KC, 2, E], F32R, att)
        bias_all = sb("bias_all", [P, NB * LC], F32, att)
        bias_now = sb("bias_now", [P, LC], F32, att)
        gate_in = sb("gate_in", [P, 2], F32, att)
        iota_i = sb("iota_i", [P, 2, E], I32, att)
        falling = sb("falling", [P, E], F32, att)
        region0 = sb("region0", [P, E], F32, att)
        stats = [sb(f"stats{n}", [P, NT, 6], F32, att) for n in range(2)]
        moments = [sb(f"moments{n}", [P, NT, 2], F32, att) for n in range(2)]
        ln_v = [sb(f"ln_v{n}", [P, NT], F32, att) for n in range(2)]
        ln_l = [sb(f"ln_l{n}", [P, NT], F32, att) for n in range(2)]
        ln_y = [sb(f"ln_y{n}", [P, NT], F32, att) for n in range(2)]
        ln_a = [sb(f"ln_a{n}", [P, NT], F32, att) for n in range(2)]
        ln_b = [sb(f"ln_b{n}", [P, NT], F32, att) for n in range(2)]
        rstd = [sb(f"rstd{n}", [P, NT], F32, att) for n in range(2)]
        shift = [sb(f"shift{n}", [P, NT], F32, att) for n in range(2)]
        neg_max = sb("neg_max", [P, NT], F32, att)
        exp_sum = sb("exp_sum", [P, NT], F32, att)
        exp_inv = sb("exp_inv", [P, NT], F32, att)
        att_scale = sb("att_scale", [P, NT], F32, att)
        logits = sb("logits", [P, NT, E], F32, att)
        below = sb("below", [P, NT, E], F32, att)
        ex = sb("ex", [P, NT, E], F32, att)
        cand = sb("cand", [P, NT, E], F32, att)
        best = sb("best", [P, NT], F32, att)
        second = sb("second", [P, NT], F32, att)
        ratio = sb("ratio", [P, NT], F32, att)
        chosen = sb("chosen", [P, 2, NT, E], F32, att)
        slot_of = sb("slot_of", [P, 2, NT, E], F32, att)
        place = sb("place", [P, NT, E], F32, att)
        e_sum = sb("e_sum", [P, NT], F32, att)
        den = sb("den", [P, NT], F32, att)
        w_first = sb("w_first", [P, NT], F32, att)
        w_second = sb("w_second", [P, NT], F32, att)
        picked = sb("picked", [P, NT, E], BF16, att)
        picked_before = sb("picked_before", [P, E], BF16, att)
        picked_now = sb("picked_now", [P, E], F32, att)
        slots = sb("slots", [P, 2 * NT], F32, att)
        slots_i = sb("slots_i", [P, 2 * NT], I32, att)
        count_f = sb("count_f", [P, E], F32, att)
        blocks_i = sb("blocks_i", [P, E], I32, att)
        block_f = sb("block_f", [P, E], F32, att)
        first_f = sb("first_f", [P, E], F32, att)
        pad_id = sb("pad_id", [P, MIN_BLOCKS, E], I32, att)

        prep = ExitStack()
        prep_in = sb("prep_in", [P, KC * NB * LC + 3 * KC * D], F32, prep)
        prep_hi = sb("prep_hi", [P, KC * NB * LC + 3 * KC * D], F32R, prep)
        prep_lo = sb("prep_lo", [P, KC * NB * LC + 3 * KC * D], F32R, prep)
        k_f = sb("k_f", [P, KC, NB * LC], F32, prep)
        k_hi = sb("k_hi", [P, KC, NB * LC], F32R, prep)
        k_lo = sb("k_lo", [P, KC, NB * LC], F32R, prep)
        v_f = sb("v_f", [P, NB * 2 * D], F32, prep)
        mask_i = sb("mask_i", [P, NB * LC], I32, prep)
        keep = sb("keep", [P, NB * LC], F32, prep)
        masked = sb("masked", [P, NB * LC], F32, prep)
        bias_cols = sb("bias_cols", [P, 2, KC], F32, prep)
        bq_hi = sb("bq_hi", [P, KC, P], F32R, prep)
        bq_lo = sb("bq_lo", [P, KC, P], F32R, prep)
        bv_row = sb("bv_row", [P, D], F32, prep)
        prep.close()
        sc = sb("sc", [P, NT, LC], F32, att)
        p_hi = [sb(f"p_hi{q}", [CH, 2, TQ * P], F32R, att) for q in range(2)]
        p_lo = [sb(f"p_lo{q}", [CH, 2, TQ * P], F32R, att) for q in range(2)]
        x_res = sb("x_res", [P, NT, D], F32, att)
        x2 = sb("x2", [P, NT, D], F32, att)
        xn2 = sb("xn2", [P, NT, D], F32, att)
        rows = sb("rows", [P, NT, ROW], F32, att)
        att.close()

        w_hi.append(sb("w_hi1", [P, WCOLS], F32R))
        w_lo.append(sb("w_lo1", [P, WCOLS], F32R))
        block_rows = sb("block_rows", [P, D], F32)
        xt_hi = sb("xt_hi", [P, KC, P], F32R)
        xt_lo = sb("xt_lo", [P, KC, P], F32R)
        u_sb = [sb(f"u_sb{h}", [P, FH], F32) for h in range(2)]
        h_sb = [sb(f"h_sb{h}", [P, FH], F32) for h in range(2)]
        ht_hi = [sb(f"ht_hi{h}", [P, FC // 2, P], F32R) for h in range(2)]
        ht_lo = [sb(f"ht_lo{h}", [P, FC // 2, P], F32R) for h in range(2)]
        weight_token = sb("weight_token", [P, 2], F32)
        y_sb = sb("y_sb", [P, D], F32)

        turned = [ps[:, 4 * q:4 * q + 2, :] for q in range(2)]
        prods = [ps[:, 4 * q + 2:4 * q + 4, :] for q in range(2)]
        logits_ps = turned[1][:, 0, 0:NT * 2 * E].rearrange("p (t two e) -> p t two e", two=2, e=E)
        ranks = turned[0][:, 0, 0:NT * E]
        g_ps = [ps[:, 0, :], ps[:, 1, :]]
        u_ps = [ps[:, 2, :], ps[:, 3, :]]
        ht_ps = [ps[:, 4, :], ps[:, 5, :]]
        xt_ps = ps[:, 6, 0:D]
        y_ps = ps[:, 7, 0:D]

        pool_waited = sem("pool_waited")
        dve_waited = sem("dve_waited")
        sp_waited = sem("sp_waited")
        prep_loaded = sem("prep_loaded")
        small_loaded = sem("small_loaded")
        x_loaded = sem("x_loaded")
        x_res_loaded = sem("x_res_loaded")
        raw_loaded = [sem(f"raw_loaded{n}") for n in range(2)]
        consts_made = sem("consts_made")
        pool_step = sem("pool_step")
        dve_step = sem("dve_step")
        act_step = sem("act_step")
        prep_split_hi = sem("prep_split_hi")
        prep_split = sem("prep_split")
        wr_split_hi = sem("wr_split_hi")
        k_made = sem("k_made")
        k_masked = sem("k_masked")
        k_split_hi = sem("k_split_hi")
        k_split = sem("k_split")
        v_made = sem("v_made")
        v_biased = sem("v_biased")
        v_split_hi = sem("v_split_hi")
        m_made = sem("m_made")
        m_split_hi = sem("m_split_hi")
        m_split = sem("m_split")
        bqk_made = sem("bqk_made")
        first_split = sem("first_split")
        var_ready = [sem(f"var_ready{n}") for n in range(2)]
        guess_ready = [sem(f"guess_ready{n}") for n in range(2)]
        rstd_ready = [sem(f"rstd_ready{n}") for n in range(2)]
        xn_ready = sem("xn_ready")
        x_turned = sem("x_turned")
        xt_split_hi = sem("xt_split_hi")
        xt_split = sem("xt_split")
        scored = sem("scored")
        maxed = sem("maxed")
        exped = sem("exped")
        p_turned = sem("p_turned")
        pt_split_hi = sem("pt_split_hi")
        pt_split = sem("pt_split")
        attended = sem("attended")
        x2_made = sem("x2_made")
        x2_stored = sem("x2_stored")
        xn2_ready = sem("xn2_ready")
        x2_turned = sem("x2_turned")
        x2t_split_hi = sem("x2t_split_hi")
        x2t_split = sem("x2t_split")
        logits_ready = sem("logits_ready")
        logits_read = sem("logits_read")
        rows_free = sem("rows_free")
        rows_filled = sem("rows_filled")
        below_ready = sem("below_ready")
        second_ready = sem("second_ready")
        route_exped = sem("route_exped")
        picked_ready = sem("picked_ready")
        ranked = sem("ranked")
        slots_ready = sem("slots_ready")
        rows_scattered = [sem(f"rows_scattered{q}") for q in range(2)]
        counted = sem("counted")
        plan_ready = sem("plan_ready")
        pads_ready = sem("pads_ready")
        pads_stored = sem("pads_stored")
        dummy_stored = sem("dummy_stored")
        block_loaded = sem("block_loaded")
        block_turned = sem("block_turned")
        bt_split_hi = sem("bt_split_hi")
        bt_split = sem("bt_split")
        gu_done = [sem(f"gu_done{h}") for h in range(2)]
        u_copied = [sem(f"u_copied{h}") for h in range(2)]
        h_made = [sem(f"h_made{h}") for h in range(2)]
        h_turned = [sem(f"h_turned{h}") for h in range(2)]
        ht_split_hi = [sem(f"ht_split_hi{h}") for h in range(2)]
        ht_split = [sem(f"ht_split{h}") for h in range(2)]
        w_split_hi = sem("w_split_hi")
        w_split = sem("w_split")
        y_done = sem("y_done")
        y_weighted = sem("y_weighted")
        meta_loaded = sem("meta_loaded")
        y_added = sem("y_added")
        y_free = sem("y_free")

        ctx_hi = prep_hi[:, 0:KC * NB * LC].rearrange("p (k n) -> p k n", k=KC)
        ctx_lo = prep_lo[:, 0:KC * NB * LC].rearrange("p (k n) -> p k n", k=KC)

        def small_w(t, n):
            o = KC * NB * LC + n * KC * D
            return t[:, o:o + KC * D].rearrange("p (k n) -> p k n", k=KC)

        x_v = x.rearrange("(b p t) d -> b p (t d)", p=P, t=NT)
        out_v = out[0:T, :].rearrange("(b p t) d -> b p (t d)", p=P, t=NT)
        block = whole.enter_context(nc.Block())

        @block.sync
        def _(sp):
            flat = lambda t: t[:].rearrange("p t d -> p (t d)")

            def load_raw(src, half):
                cols = slice(half * WCOLS // 2, (half + 1) * WCOLS // 2)
                sp.dma_start(w_raw[:, cols], src[:, cols]).then_inc(raw_loaded[half], 16)

            sp.dma_start(prep_in[:], w_small).then_inc(prep_loaded, 16)
            sp.dma_start(mask_i[:], mask.partition_broadcast(P)).then_inc(small_loaded, 16)
            sp.dma_start(bias_cols[:, 0, :], bq).then_inc(small_loaded, 16)
            sp.dma_start(bias_cols[:, 1, :], bk).then_inc(small_loaded, 16)
            sp.dma_start(bv_row[:], bv.partition_broadcast(P)).then_inc(small_loaded, 16)
            sp.dma_start(gate_in[:], gates.partition_broadcast(P)).then_inc(small_loaded, 16)
            sp.dma_start(wr_f[:].rearrange("p k e -> p (k e)"), wr_t).then_inc(small_loaded, 16)
            sp.dma_start(flat(x_ln), x_v[0]).then_inc(x_loaded, 16)
            load_raw(w_experts[0], 0)
            load_raw(w_experts[0], 1)
            sp.wait_ge(pads_ready, 1)
            sp.dma_start(out[T:T + P, :], pads[:, 0, 0:D]).then_inc(dummy_stored, 16)
            sp.wait_ge(m_split, 1)
            sp.dma_start(flat(x_res), x_v[0]).then_inc(x_res_loaded, 16)
            sp.wait_ge(x_turned, 2)
            sp.dma_start(flat(x_ln), x_v[1]).then_inc(x_loaded, 16)

            def store_x2(b):
                sp.wait_ge(x2_made, b * 2 + 2)
                sp.sem_inc(sp_waited)
                sp.dma_start(out_v[bass.ds(b, 1)].squeeze(0), flat(x2)).then_inc(x2_stored, 16)

            def load_res(b):
                sp.dma_start(flat(x_res), x_v[bass.ds(b, 1)].squeeze(0)).then_inc(x_res_loaded, 16)

            with sp.Fori(0, NB - 2) as i:
                store_x2(i)
                load_res(i + 1)
                sp.wait_ge(x_turned, i * 2 + 4)
                sp.sem_inc(sp_waited)
                sp.dma_start(flat(x_ln), x_v[bass.ds(i + 2, 1)].squeeze(0)).then_inc(x_loaded, 16)
            store_x2(NB - 2)
            load_res(NB - 1)
            store_x2(NB - 1)

            sp.wait_ge(first_split, 1)
            load_raw(w_experts[1], 0)
            load_raw(w_experts[1], 1)

            sp.wait_ge(plan_ready, 1)
            for e in range(E):
                n = sp.value_load(count_row[0:1, e:e + 1], min_val=0, max_val=T)
                at = n + e * REGION
                sp.dma_start(rows_dram[bass.ds(at, PAD), :].rearrange("(p k) c -> p (k c)", p=P),
                             pads[:].rearrange("p k c -> p (k c)")).then_inc(pads_stored, 16)
            sp.wait_ge(pads_stored, 16 * E)
            for q in range(2):
                sp.wait_ge(rows_scattered[q], SCATTERED * NB)

            def load_block(row, blk):
                sp.wait_ge(block_turned, blk + FREE)
                sp.sem_inc(sp_waited)
                sp.dma_start(block_rows[:], rows_dram[bass.ds(row, P), 0:D]).then_inc(block_loaded, 16)

            load_block(0, 0)
            with sp.Fori(0, E // 2) as pair:
                for odd in range(2):
                    e = pair * 2 + odd
                    n = sp.value_load(last_row[0:1, bass.ds(e, 1)], min_val=MIN_BLOCKS - 1, max_val=T // P - 1)
                    b0 = sp.value_load(first_row[0:1, bass.ds(e, 1)], min_val=0, max_val=T)
                    load_block(e * REGION + P, b0 + 1)
                    load_block(e * REGION + 2 * P, b0 + 2)
                    after = w_experts[bass.ds((e + 2) & (E - 1), 1)].squeeze(0)
                    sp.wait_ge(w_split, e * PIECES + PIECES // 2 + FREE)
                    sp.sem_inc(sp_waited)
                    load_raw(after, 0)
                    with sp.Fori(3, n + 1) as j:
                        load_block(e * REGION + j * P, b0 + j)
                    load_block(((e + 1) & (E - 1)) * REGION, b0 + n + 1)
                    sp.wait_ge(w_split, e * PIECES + PIECES + FREE)
                    sp.sem_inc(sp_waited)
                    load_raw(after, 1)
            for half in range(2):
                sp.wait_ge(raw_loaded[half], 16 * (E + 2))
            sp.wait_ge(x_loaded, 16 * NB)
            sp.wait_ge(x_res_loaded, 16 * NB)
            sp.wait_ge(x2_stored, 16 * NB)
            sp.wait_ge(dummy_stored, 16)

        @block.gpsimd
        def _(pool):
            step = Steps(pool, pool_step)
            for s in (*h_made, *ht_split, slots_ready, block_turned, bt_split, w_split, y_done, y_weighted,
                      y_free):
                pool.sem_inc(s, FREE)
            pool.memset(ident[:], 0.0)
            pool.memset(earlier[:], 1.0)
            pool.memset(ones[:], 1.0)
            pool.memset(picked_before[:], 0.0)
            pool.iota(iota_i[:, 0, :], [[-1, E]], base=E, channel_multiplier=0)
            pool.iota(iota_i[:, 1, :], [[REGION, E]], base=0, channel_multiplier=0)
            pool.iota(pad_id[:], [[1, MIN_BLOCKS], [0, E]], base=0, channel_multiplier=MIN_BLOCKS)
            row_words = rows[:, :, D:ROW].bitcast(I32).rearrange("p t (e two) -> p t e two", two=2)[:, :, :, 1]
            step.mark(pool.memset(pads[:], 0.0))
            step.settle()
            pool.affine_select(out=ident[:], in_=ident[:], compare_op=ALU.not_equal, fill=1.0, base=0,
                               pattern=[[-1, P]], channel_multiplier=1)
            pool.affine_select(out=earlier[:], in_=earlier[:], compare_op=ALU.is_gt, fill=0.0, base=0,
                               pattern=[[1, P]], channel_multiplier=-1).then_inc(consts_made, 1)

            for c in range(PIECES):
                if c % (PIECES // 2) == 0:
                    pool.wait_ge(raw_loaded[c // (PIECES // 2)], 16)
                cols = slice(c * PIECE, (c + 1) * PIECE)
                step.mark(pool.tensor_scalar(w_hi[0][:, cols], w_raw[:, cols], 1.0, None, ALU.mult))
            step.settle()
            for c in range(PIECES):
                cols = slice(c * PIECE, (c + 1) * PIECE)
                last = pool.tensor_tensor(w_lo[0][:, cols], w_raw[:, cols], w_hi[0][:, cols].bitcast(F32),
                                          ALU.subtract)
            last.then_inc(first_split, 1)

            pool.wait_ge(m_split, 1)
            step.mark(pool.iota(row_words, [[1, NT], [0, E]], base=-S, channel_multiplier=NT))
            step.settle()

            def number_rows():
                step.mark(pool.tensor_scalar(row_words, row_words, float(S), None, ALU.add))
                step.settle()
                pool.sem_inc(rows_free)

            def scatter(b):
                pool.wait_ge(slots_ready, b + 1 + FREE)
                pool.wait_ge(rows_filled, b + 1)
                pool.sem_inc(pool_waited)
                for q in range(2):
                    for t in range(q * TQ, (q + 1) * TQ):
                        for k in range(2):
                            pool.indirect_dma_start(
                                rows_dram,
                                bass.IndirectOffsetOnAxis(ap=slots_i[:, k * NT + t:k * NT + t + 1], axis=0),
                                rows[:, t, :], None).then_inc(rows_scattered[q], 16)

            number_rows()
            scatter(0)
            with pool.Fori(1, NB) as i:
                step.loop(i - 1, 1)
                for q in range(2):
                    pool.wait_ge(rows_scattered[q], i * SCATTERED)
                pool.sem_inc(pool_waited)
                number_rows()
                scatter(i)
            step.leave(NB - 1)

            pool.wait_ge(plan_ready, 1)
            pool.wait_ge(pads_stored, 16 * E)
            for q in range(2):
                pool.wait_ge(rows_scattered[q], SCATTERED * NB)
            pool.wait_ge(x2_stored, 16 * NB)
            pool.wait_ge(dummy_stored, 16)
            with pool.Fori(0, E) as e:
                n = pool.value_load(last_row[0:1, bass.ds(e, 1)], min_val=MIN_BLOCKS - 1, max_val=T // P - 1)
                b0 = pool.value_load(first_row[0:1, bass.ds(e, 1)], min_val=0, max_val=T)
                with pool.Fori(0, n + 1) as j:
                    pool.dma_start(weight_token[:],
                                   rows_dram[bass.ds(e * REGION + j * P, P), bass.ds(e * 2 + D, 2)]
                                   ).then_inc(meta_loaded, 16)
                    pool.wait_ge(meta_loaded, (b0 + j) * 16 + 16)
                    pool.wait_ge(y_weighted, b0 + j + 1 + FREE)
                    pool.sem_inc(pool_waited)
                    pool.indirect_dma_start(
                        out, bass.IndirectOffsetOnAxis(ap=weight_token[:, 1:2].bitcast(I32), axis=0),
                        y_sb[:], None, compute_op=ALU.add).then_inc(y_added, 16)
                    pool.wait_ge(y_added, (b0 + j) * 16 + 16)
                    pool.sem_inc(y_free)

        @block.scalar
        def _(act):
            step = Steps(act, act_step)
            act.wait_ge(small_loaded, 16 * 6)
            step.mark(act.activation(gate[:], gate_in[:], ACT.Tanh))
            act.copy(wr_pair[:, :, 0, :], wr_f[:]).then_inc(wr_split_hi, 1)
            act.wait_ge(prep_loaded, 16)
            act.copy(prep_hi[:], prep_in[:]).then_inc(prep_split_hi, 1)
            act.preload_act_table_set("natural_log_exp_and_others")
            act.wait_ge(k_masked, 1)
            act.copy(k_hi[:], k_f[:]).then_inc(k_split_hi, 1)
            act.wait_ge(v_biased, 1)
            act.copy(v_hi[0:CH, :], v_f[0:CH, :]).then_inc(v_split_hi, 1)
            act.wait_ge(m_made, 1)
            for m in range(KC):
                last = act.copy(m_hi[:, m * NB * LC:(m + 1) * NB * LC].rearrange("p (h n) -> p h n", h=2),
                                ps[:, 2 * m:2 * m + 2, 0:2 * LC])
            last.then_inc(m_split_hi, 1)

            def guess_rstd(n, b):
                act.wait_ge(var_ready[n], b + 1)
                step.mark(act.activation(ln_l[n][:], ln_v[n][:], ACT.Ln))
                step.settle()
                act.activation(ln_y[n][:], ln_l[n][:], ACT.Exp, scale=-0.5).then_inc(guess_ready[n], 1)

            def normalise(n, b, source, result, ready):
                act.wait_ge(rstd_ready[n], b + 1)
                for q in range(2):
                    for t in range(q * TQ, (q + 1) * TQ):
                        last = act.activation(result[:, t, :], source[:, t, :], ACT.Identity,
                                              bias=shift[n][:, t:t + 1], scale=rstd[n][:, t:t + 1])
                    last.then_inc(ready, 1)

            def split_turned(b, ready, result, rows_of, split):
                for q in range(2):
                    act.wait_ge(ready, b * 2 + q + 1)
                    act.copy(result[q][:], turned[q][0:rows_of]).then_inc(split, 1)

            def exps(b):
                for q in range(2):
                    act.wait_ge(maxed, b * 2 + q + 1)
                    for t in range(q * TQ, (q + 1) * TQ):
                        last = act.activation(sc[:, t, :], sc[:, t, :], ACT.Exp, bias=neg_max[:, t:t + 1],
                                              scale=-1.0, accum_out=exp_sum[:, t:t + 1])
                    last.then_inc(exped, 1)

            def route_exps(b):
                act.wait_ge(below_ready, b + 1)
                act.activation(ex[:], below[:], ACT.Exp)
                act.wait_ge(second_ready, b + 1)
                act.activation(ratio[:], second[:], ACT.Exp).then_inc(route_exped, 1)

            def fill_rows(b):
                act.wait_ge(rows_free, b + 1)
                act.copy(rows[:, :, 0:D], xn2[:]).then_inc(rows_filled, 1)

            def attend_and_route(a, b, l):
                if a is not None:
                    split_turned(a, x_turned, t_hi, P, xt_split_hi)
                if b is not None:
                    guess_rstd(1, b)
                    normalise(1, b, x2, xn2, xn2_ready)
                if a is not None:
                    exps(a)
                if b is not None:
                    split_turned(b, x2_turned, t_hi, P, x2t_split_hi)
                if l is not None:
                    guess_rstd(0, l)
                if a is not None:
                    split_turned(a, p_turned, p_hi, CH, pt_split_hi)
                if l is not None:
                    normalise(0, l, x_ln, x_ln, xn_ready)
                if b is not None:
                    route_exps(b)
                    fill_rows(b)

            guess_rstd(0, 0)
            normalise(0, 0, x_ln, x_ln, xn_ready)
            attend_and_route(0, None, 1)
            with act.Fori(0, NB - 2) as i:
                step.loop(i, 2)
                attend_and_route(i + 1, i, i + 2)
            step.leave(NB - 2)
            attend_and_route(NB - 1, NB - 2, None)
            attend_and_route(None, NB - 1, None)

            act.wait_ge(plan_ready, 1)

            def piece(e, odd, c):
                cols = slice(c * PIECE, (c + 1) * PIECE)
                act.copy(w_hi[1 - odd][:, cols], w_raw[:, cols]).then_inc(w_split_hi, 1)

            def copy_u(h, blk):
                act.wait_ge(gu_done[h], blk + 1)
                act.copy(u_sb[h][:], u_ps[h]).then_inc(u_copied[h], 1)

            def split_h(h, blk):
                act.wait_ge(h_turned[h], blk + 1)
                act.copy(ht_hi[h][:].rearrange("p c t -> p (c t)"), ht_ps[h]).then_inc(ht_split_hi[h], 1)

            def split_x(blk):
                act.wait_ge(block_turned, blk + 1 + FREE)
                act.copy(xt_hi[:].rearrange("p k t -> p (k t)"), xt_ps).then_inc(bt_split_hi, 1)

            split_x(0)
            with act.Fori(0, E // 2) as pair:
                for odd in range(2):
                    e = pair * 2 + odd
                    n = act.value_load(last_row[0:1, bass.ds(e, 1)], min_val=MIN_BLOCKS - 1, max_val=T // P - 1)
                    b0 = act.value_load(first_row[0:1, bass.ds(e, 1)], min_val=0, max_val=T)
                    copy_u(0, b0)
                    act.wait_ge(raw_loaded[0], e * 16 + 32)
                    act.wait_ge(y_done, b0 + FREE)
                    piece(e, odd, 0)
                    piece(e, odd, 1)
                    copy_u(1, b0)
                    split_x(b0 + 1)
                    split_h(0, b0)
                    piece(e, odd, 2)
                    act.wait_ge(raw_loaded[1], e * 16 + 32)
                    piece(e, odd, 3)
                    copy_u(0, b0 + 1)
                    split_h(1, b0)
                    piece(e, odd, 4)
                    copy_u(1, b0 + 1)
                    split_x(b0 + 2)
                    split_h(0, b0 + 1)
                    piece(e, odd, 5)
                    with act.Fori(1, n) as j:
                        copy_u(0, b0 + j + 1)
                        split_h(1, b0 + j)
                        copy_u(1, b0 + j + 1)
                        split_x(b0 + j + 2)
                        split_h(0, b0 + j + 1)
                    split_h(1, b0 + n)

        @block.vector
        def _(dve):
            step = Steps(dve, dve_step)

            dve.wait_ge(small_loaded, 16 * 6)
            dve.wait_ge(consts_made, 1)
            dve.tensor_scalar(keep[:], mask_i[:], 0.0, None, ALU.not_equal)
            dve.tensor_copy(bq_hi[:], bias_cols[:, 0, :].unsqueeze(2).broadcast_to([P, KC, P]))
            dve.tensor_copy(falling[:], iota_i[:, 0, :])
            dve.tensor_copy(region0[:], iota_i[:, 1, :])
            dve.wait_ge(wr_split_hi, 1)
            dve.tensor_tensor(wr_pair[:, :, 1, :], wr_f[:], wr_pair[:, :, 0, :].bitcast(F32), ALU.subtract)
            step.mark(dve.tensor_scalar(pad_id[:], pad_id[:], P - 1, None, ALU.bitwise_and))
            step.settle()
            pad_words = pads[:, :, D:ROW].bitcast(I32).rearrange("p k (e two) -> p k e two", two=2)[:, :, :, 1]
            dve.tensor_scalar(pad_words, pad_id[:], float(T), None, ALU.add).then_inc(pads_ready, 1)
            dve.tensor_scalar(masked[:], keep[:], -MASKED, MASKED, ALU.mult, ALU.add)
            dve.tensor_tensor(bq_lo[:], bias_cols[:, 0, :].unsqueeze(2).broadcast_to([P, KC, P]),
                              bq_hi[:].bitcast(F32), ALU.subtract)
            dve.wait_ge(prep_split_hi, 1)
            dve.tensor_tensor(prep_lo[:], prep_in[:], prep_hi[:].bitcast(F32), ALU.subtract
                              ).then_inc(prep_split, 1)
            dve.wait_ge(k_made, 1)
            for m in range(KC):
                for h in range(2):
                    cols = slice(h * 2 * LC, (h + 1) * 2 * LC)
                    last = dve.scalar_tensor_tensor(k_f[:, m, cols], ps[:, 2 * m + h, 0:2 * LC],
                                                    bias_cols[:, 1, m:m + 1], keep[:, cols], ALU.add, ALU.mult)
            last.then_inc(k_masked, 1)
            dve.wait_ge(k_split_hi, 1)
            dve.tensor_tensor(k_lo[:], k_f[:], k_hi[:].bitcast(F32), ALU.subtract).then_inc(k_split, 1)
            dve.wait_ge(v_made, 1)
            dve.tensor_tensor(v_f[0:CH, :].rearrange("p (n d) -> p n d", d=D),
                              ps[0:CH, 4:8, :].rearrange("p k (n d) -> p (k n) d", d=D),
                              bv_row[0:CH, :].unsqueeze(1).broadcast_to([CH, 2 * NB, D]), ALU.add
                              ).then_inc(v_biased, 1)
            dve.wait_ge(v_split_hi, 1)
            dve.tensor_tensor(v_lo[0:CH, :], v_f[0:CH, :], v_hi[0:CH, :].bitcast(F32), ALU.subtract)
            dve.wait_ge(m_split_hi, 1)
            for m in range(KC):
                cols = slice(m * NB * LC, (m + 1) * NB * LC)
                last = dve.tensor_tensor(m_lo[:, cols].rearrange("p (h n) -> p h n", h=2),
                                         ps[:, 2 * m:2 * m + 2, 0:2 * LC],
                                         m_hi[:, cols].bitcast(F32).rearrange("p (h n) -> p h n", h=2), ALU.subtract)
            dve.wait_ge(bqk_made, 1)
            dve.tensor_tensor(bias_all[:].rearrange("p (h n) -> p h n", h=2), ps[:, 4:6, 0:2 * LC],
                              masked[:].rearrange("p (h n) -> p h n", h=2), ALU.add).then_inc(m_split, 1)
            dve.wait_ge(m_split, 1)
            step.mark(dve.memset(picked_now[:], 0.0))

            def stats_of(n, b, source):
                for t in range(NT):
                    step.mark(dve.bn_stats(stats[n][:, t, :], source[:, t, :]))
                step.settle()
                dve.sem_inc(dve_waited)
                for t in range(NT):
                    step.mark(dve.bn_aggr(moments[n][:, t, :], stats[n][:, t, :]))
                step.settle()
                dve.tensor_scalar(ln_v[n][:], moments[n][:, :, 1], LN_EPS, None, ALU.add).then_inc(var_ready[n], 1)

            def newton(n, b):
                dve.wait_ge(guess_ready[n], b + 1)
                step.mark(dve.scalar_tensor_tensor(ln_a[n][:], ln_v[n][:], -0.5, ln_y[n][:], ALU.mult, ALU.mult))
                step.settle()
                step.mark(dve.tensor_tensor(ln_b[n][:], ln_a[n][:], ln_y[n][:], ALU.mult))
                step.settle()
                step.mark(dve.scalar_tensor_tensor(rstd[n][:], ln_b[n][:], 1.5, ln_y[n][:], ALU.add, ALU.mult))
                step.settle()
                dve.scalar_tensor_tensor(shift[n][:], moments[n][:, :, 0], -1.0, rstd[n][:], ALU.mult, ALU.mult
                                         ).then_inc(rstd_ready[n], 1)

            def split_turned(b, q, split_hi, lo, hi, rows_of, split):
                dve.wait_ge(split_hi, b * 2 + q + 1)
                dve.tensor_tensor(lo[q][:], turned[q][0:rows_of], hi[q][:].bitcast(F32), ALU.subtract
                                  ).then_inc(split, 1)

            def scores(b):
                step.mark(dve.tensor_copy(bias_now[:], bias_all[:, bass.ds(b * LC, LC)]))
                step.settle()
                for q in range(2):
                    dve.wait_ge(scored, b * 2 + q + 1)
                    dve.sem_inc(dve_waited)
                    for t in range(TQ):
                        last = dve.tensor_tensor_reduce(
                            out=sc[:, q * TQ + t, :], in0=prods[q][:, t // 2, (t % 2) * D:(t % 2) * D + LC],
                            in1=bias_now[:], scale=-float(D) ** -0.5, scalar=3e38, op0=ALU.add, op1=ALU.min,
                            accum_out=neg_max[:, q * TQ + t:q * TQ + t + 1])
                    last.then_inc(maxed, 1)

            def residual(b):
                step.mark(dve.reciprocal(exp_inv[:], exp_sum[:]))
                step.settle()
                step.mark(dve.tensor_scalar(att_scale[:], exp_inv[:], gate[:, 0:1], None, ALU.mult))
                step.settle()
                dve.wait_ge(x_res_loaded, b * 16 + 16)
                for q in range(2):
                    dve.wait_ge(attended, b * 2 + q + 1)
                    for t in range(q * TQ, (q + 1) * TQ):
                        last = dve.scalar_tensor_tensor(
                            x2[:, t, :], prods[q][:, (t % TQ) // 2, (t % 2) * D:(t % 2 + 1) * D],
                            att_scale[:, t:t + 1], x_res[:, t, :], ALU.mult, ALU.add)
                    last.then_inc(x2_made, 1)

            def read_logits(b):
                dve.wait_ge(logits_ready, b + 1)
                dve.tensor_reduce(logits[:], logits_ps.rearrange("p t two e -> p t e two"), AX.X, ALU.add
                                  ).then_inc(logits_read, 1)

            def choose_experts(b):
                lg = logits[:]
                fall = falling[:].unsqueeze(1).broadcast_to([P, NT, E])
                dve.wait_ge(logits_read, b + 1)
                step.mark(dve.tensor_reduce(best[:], lg, AX.X, ALU.max))
                step.settle()
                dve.tensor_tensor(below[:], lg, best[:].unsqueeze(2).broadcast_to([P, NT, E]), ALU.subtract
                                  ).then_inc(below_ready, 1)
                dve.wait_ge(below_ready, b + 1)

                def choose(k):
                    step.mark(dve.tensor_reduce(best[:], cand[:], AX.X, ALU.max))
                    step.settle()
                    step.mark(dve.tensor_tensor(chosen[:, k], cand[:],
                                                best[:].unsqueeze(2).broadcast_to([P, NT, E]), ALU.is_equal))
                    step.settle()

                step.mark(dve.tensor_scalar(cand[:], below[:], 0.0, None, ALU.is_ge))
                step.settle()
                step.mark(dve.tensor_tensor(cand[:], cand[:], fall, ALU.mult))
                step.settle()
                choose(0)
                step.mark(dve.scalar_tensor_tensor(place[:].rearrange("p t e -> p (t e)"),
                                                   chosen[:, 0].rearrange("p t e -> p (t e)"), BELOW,
                                                   below[:].rearrange("p t e -> p (t e)"), ALU.mult, ALU.add))
                step.settle()
                dve.tensor_reduce(second[:], place[:], AX.X, ALU.max).then_inc(second_ready, 1)
                dve.wait_ge(second_ready, b + 1)
                step.mark(dve.tensor_tensor(cand[:], place[:], second[:].unsqueeze(2).broadcast_to([P, NT, E]),
                                            ALU.is_ge))
                step.settle()
                step.mark(dve.tensor_tensor(cand[:], cand[:], fall, ALU.mult))
                step.settle()
                choose(1)
                dve.tensor_tensor(picked[:], chosen[:, 0], chosen[:, 1], ALU.add).then_inc(picked_ready, 1)
                dve.wait_ge(route_exped, b + 1)
                step.mark(dve.tensor_reduce(e_sum[:], ex[:], AX.X, ALU.add))
                step.settle()
                step.mark(dve.scalar_tensor_tensor(den[:], e_sum[:], K_EPS, ratio[:], ALU.mult, ALU.add))
                step.settle()
                step.mark(dve.tensor_scalar(den[:], den[:], 1.0, None, ALU.add))
                step.settle()
                step.mark(dve.reciprocal(w_first[:], den[:]))
                step.settle()
                step.mark(dve.tensor_scalar(w_first[:], w_first[:], gate[:, 1:2], None, ALU.mult))
                step.settle()
                step.mark(dve.tensor_tensor(w_second[:], w_first[:], ratio[:], ALU.mult))
                step.settle()
                dve.tensor_tensor(cand[:], chosen[:, 0], w_first[:].unsqueeze(2).broadcast_to([P, NT, E]), ALU.mult)
                step.mark(dve.tensor_tensor(place[:], chosen[:, 1],
                                            w_second[:].unsqueeze(2).broadcast_to([P, NT, E]), ALU.mult))
                step.settle()

            def find_slots(b):
                dve.wait_ge(rows_free, b + 1)
                row_weights = rows[:, :, D:ROW].rearrange("p t (e two) -> p t e two", two=2)[:, :, :, 0]
                step.mark(dve.tensor_tensor(row_weights, cand[:], place[:], ALU.add))
                step.settle()
                dve.wait_ge(ranked, b + 1)
                step.mark(dve.tensor_tensor(place[:], ranks.rearrange("p (t e) -> p t e", e=E),
                                            region0[:].unsqueeze(1).broadcast_to([P, NT, E]), ALU.add))
                step.mark(dve.tensor_reduce(picked_now[:], picked[:].rearrange("p t e -> p e t"), AX.X, ALU.add))
                step.settle()
                step.mark(dve.tensor_tensor(slot_of[:, 0], chosen[:, 0], place[:], ALU.mult))
                step.mark(dve.tensor_tensor(slot_of[:, 1], chosen[:, 1], place[:], ALU.mult))
                step.mark(dve.tensor_tensor(picked_before[:], picked_before[:], picked_now[:], ALU.add))
                step.settle()
                step.mark(dve.tensor_reduce(slots[:], slot_of[:].rearrange("p k t e -> p (k t) e"), AX.X, ALU.add))
                step.settle()
                dve.tensor_copy(slots_i[:], slots[:]).then_inc(slots_ready, 1)

            def attend_and_route(a, b, l):
                if b is not None:
                    dve.wait_ge(x2_made, b * 2 + 2)
                    stats_of(1, b, x2)
                if a is not None:
                    for q in range(2):
                        split_turned(a, q, xt_split_hi, t_lo, t_hi, P, xt_split)
                if b is not None:
                    newton(1, b)
                if a is not None:
                    scores(a)
                if l is not None:
                    dve.wait_ge(x_loaded, l * 16 + 16)
                    stats_of(0, l, x_ln)
                if b is not None:
                    for q in range(2):
                        split_turned(b, q, x2t_split_hi, t_lo, t_hi, P, x2t_split)
                if l is not None:
                    newton(0, l)
                if a is not None:
                    split_turned(a, 0, pt_split_hi, p_lo, p_hi, CH, pt_split)
                if b is not None:
                    read_logits(b)
                if a is not None:
                    split_turned(a, 1, pt_split_hi, p_lo, p_hi, CH, pt_split)
                if b is not None:
                    choose_experts(b)
                if a is not None:
                    if b is not None:
                        dve.wait_ge(x2_stored, b * 16 + 16)
                        dve.wait_ge(xn2_ready, b * 2 + 2)
                    residual(a)
                if b is not None:
                    find_slots(b)

            dve.wait_ge(x_loaded, 16)
            stats_of(0, 0, x_ln)
            newton(0, 0)
            attend_and_route(0, None, 1)
            with dve.Fori(0, NB - 2) as i:
                step.loop(i, DVE_STEPS)
                attend_and_route(i + 1, i, i + 2)
            step.leave(NB - 2)
            attend_and_route(NB - 1, NB - 2, None)
            attend_and_route(None, NB - 1, None)

            dve.wait_ge(counted, 1)
            dve.tensor_copy(count_row[:], ranks[:, 0:E])
            step.mark(dve.tensor_scalar(blocks_i[:], ranks[:, 0:E], float(P - 1), None, ALU.add))
            step.settle()
            step.mark(dve.tensor_scalar(blocks_i[:], blocks_i[:], P.bit_length() - 1, None,
                                        ALU.logical_shift_right))
            step.settle()
            step.mark(dve.tensor_scalar(block_f[:], blocks_i[:], float(MIN_BLOCKS), None, ALU.max))
            step.settle()
            step.mark(dve.tensor_scalar(last_row[:], block_f[:], -1.0, None, ALU.add))
            step.mark(dve.memset(first_f[:], 0.0))
            step.settle()
            for e in range(1, E):
                step.mark(dve.tensor_tensor(first_f[:, e:e + 1], first_f[:, e - 1:e], block_f[:, e - 1:e], ALU.add))
                step.settle()
            dve.tensor_copy(first_row[:], first_f[:]).then_inc(plan_ready, 1)
            dve.wait_ge(plan_ready, 1)

            def piece(e, odd, c):
                cols = slice(c * PIECE, (c + 1) * PIECE)
                dve.wait_ge(w_split_hi, e * PIECES + (c + 1))
                dve.tensor_tensor(w_lo[1 - odd][:, cols], w_raw[:, cols], w_hi[1 - odd][:, cols].bitcast(F32),
                                  ALU.subtract).then_inc(w_split, 1)

            def make_h(h, blk):
                dve.wait_ge(u_copied[h], blk + 1)
                dve.scalar_tensor_tensor(h_sb[h][:], g_ps[h], 0.0, u_sb[h][:], ALU.max, ALU.mult
                                         ).then_inc(h_made[h], 1)

            def split_h(h, blk):
                dve.wait_ge(ht_split_hi[h], blk + 1)
                dve.tensor_tensor(ht_lo[h][:].rearrange("p c t -> p (c t)"), ht_ps[h],
                                  ht_hi[h][:].bitcast(F32).rearrange("p c t -> p (c t)"), ALU.subtract
                                  ).then_inc(ht_split[h], 1)

            def split_x(blk):
                dve.wait_ge(bt_split_hi, blk + 1)
                dve.tensor_tensor(xt_lo[:].rearrange("p k t -> p (k t)"), xt_ps,
                                  xt_hi[:].bitcast(F32).rearrange("p k t -> p (k t)"), ALU.subtract
                                  ).then_inc(bt_split, 1)

            def weigh_y(blk):
                dve.wait_ge(y_done, blk + 1 + FREE)
                dve.wait_ge(meta_loaded, blk * 16 + 16)
                dve.wait_ge(y_free, blk + FREE)
                dve.tensor_scalar(y_sb[:], y_ps, weight_token[:, 0:1], None, ALU.mult).then_inc(y_weighted, 1)

            split_x(0)
            with dve.Fori(0, E // 2) as pair:
                for odd in range(2):
                    e = pair * 2 + odd
                    n = dve.value_load(last_row[0:1, bass.ds(e, 1)], min_val=MIN_BLOCKS - 1, max_val=T // P - 1)
                    b0 = dve.value_load(first_row[0:1, bass.ds(e, 1)], min_val=0, max_val=T)
                    make_h(0, b0)
                    piece(e, odd, 0)
                    make_h(1, b0)
                    split_x(b0 + 1)
                    split_h(0, b0)
                    piece(e, odd, 1)
                    piece(e, odd, 2)
                    make_h(0, b0 + 1)
                    split_h(1, b0)
                    piece(e, odd, 3)
                    piece(e, odd, 4)
                    make_h(1, b0 + 1)
                    split_x(b0 + 2)
                    split_h(0, b0 + 1)
                    weigh_y(b0)
                    piece(e, odd, 5)
                    with dve.Fori(1, n) as j:
                        make_h(0, b0 + j + 1)
                        split_h(1, b0 + j)
                        make_h(1, b0 + j + 1)
                        split_x(b0 + j + 2)
                        split_h(0, b0 + j + 1)
                        weigh_y(b0 + j)
                    split_h(1, b0 + n)
                    weigh_y(b0 + n)

        @block.tensor
        def _(pe):
            def product(o, lhs, rhs, first, last):
                pe.matmul(o, lhs[0], rhs[0], start=first, stop=False)
                pe.matmul(o, lhs[0], rhs[1], start=False, stop=False)
                return pe.matmul(o, lhs[1], rhs[0], start=False, stop=last)

            wk = [small_w(t, 0) for t in (prep_hi, prep_lo)]
            wv = [small_w(t, 1) for t in (prep_hi, prep_lo)]
            wq = [small_w(t, 2) for t in (prep_hi, prep_lo)]
            ctx = [ctx_hi, ctx_lo]
            kk = [k_hi, k_lo]
            pe.wait_ge(prep_split, 1)
            for m in range(KC):
                for h in range(2):
                    for k in range(KC):
                        last = product(ps[:, 2 * m + h, 0:2 * LC], [w[:, k, m * P:(m + 1) * P] for w in wk],
                                       [c[:, k, h * 2 * LC:(h + 1) * 2 * LC] for c in ctx], k == 0, k == KC - 1)
            last.then_inc(k_made, 1)
            for n in range(2 * NB):
                for k in range(KC):
                    last = product(ps[0:CH, 4 + n // 2, (n % 2) * D:(n % 2 + 1) * D],
                                   [c[:, k, n * CH:(n + 1) * CH] for c in ctx], [w[:, k, :] for w in wv],
                                   k == 0, k == KC - 1)
            last.then_inc(v_made, 1)
            pe.wait_ge(k_split, 1)
            for m in range(KC):
                for h in range(2):
                    for k in range(KC):
                        last = product(ps[:, 2 * m + h, 0:2 * LC], [w[:, k, m * P:(m + 1) * P] for w in wq],
                                       [t[:, k, h * 2 * LC:(h + 1) * 2 * LC] for t in kk], k == 0, k == KC - 1)
            last.then_inc(m_made, 1)
            pe.wait_ge(v_biased, 1)
            for h in range(2):
                for k in range(KC):
                    last = product(ps[:, 4 + h, 0:2 * LC], [t[:, k, :] for t in (bq_hi, bq_lo)],
                                   [t[:, k, h * 2 * LC:(h + 1) * 2 * LC] for t in kk], k == 0, k == KC - 1)
            last.then_inc(bqk_made, 1)
            pe.wait_ge(m_split, 1)
            pe.wait_ge(consts_made, 1)

            tt = [[t_hi[q], t_lo[q]] for q in range(2)]

            def turn_tokens(b, source, ready, done):
                for q in range(2):
                    pe.wait_ge(ready, b * 2 + q + 1)
                    for k in range(KC):
                        for t in range(TQ):
                            last = pe.transpose(turned[q][:, k, t * P:(t + 1) * P],
                                                source[:, q * TQ + t, k * P:(k + 1) * P], ident[:])
                    last.then_inc(done, 1)

            def scores(b):
                for q in range(2):
                    pe.wait_ge(xt_split, b * 2 + q + 1)
                    for t in range(TQ):
                        for k in range(KC):
                            last = product(prods[q][:, t // 2, (t % 2) * D:(t % 2) * D + LC],
                                           [a[:, k, t * P:(t + 1) * P] for a in tt[q]],
                                           [m[:, bass.ds(b * LC + k * NB * LC, LC)] for m in (m_hi, m_lo)],
                                           k == 0, k == KC - 1)
                    last.then_inc(scored, 1)

            def turn_exps(b, q):
                pe.wait_ge(exped, b * 2 + q + 1)
                for c in range(2):
                    for t in range(TQ):
                        last = pe.transpose(turned[q][0:CH, c, t * P:(t + 1) * P],
                                            sc[:, q * TQ + t, c * CH:(c + 1) * CH], ident[:])
                last.then_inc(p_turned, 1)

            def attention(b):
                for q in range(2):
                    pe.wait_ge(pt_split, b * 2 + q + 1)
                    for t in range(TQ):
                        for c in range(2):
                            last = product(prods[q][:, t // 2, (t % 2) * D:(t % 2 + 1) * D],
                                           [a[:, c, t * P:(t + 1) * P] for a in (p_hi[q], p_lo[q])],
                                           [v[0:CH, bass.ds(b * (2 * D) + c * D, D)] for v in (v_hi, v_lo)],
                                           c == 0, c == 1)
                    last.then_inc(attended, 1)

            def router_logits(b):
                for q in range(2):
                    for t in range(TQ):
                        for k in range(KC):
                            hi, lo = [a[:, k, t * P:(t + 1) * P] for a in tt[q]]
                            pe.matmul(logits_ps[:, q * TQ + t].rearrange("p two e -> p (two e)"), hi,
                                      wr_pair[:, k].rearrange("p two e -> p (two e)"),
                                      start=k == 0, stop=False)
                            last = pe.matmul(logits_ps[:, q * TQ + t, 0, :], lo, wr_pair[:, k, 0, :],
                                             start=False, stop=k == KC - 1)
                last.then_inc(logits_ready, 1)

            def rank_tokens(b):
                pe.wait_ge(picked_ready, b + 1)
                flat = picked[:].rearrange("p t e -> p (t e)")
                pe.matmul(ranks, earlier[:], flat, start=True, stop=False)
                pe.matmul(ranks.rearrange("p (t e) -> p t e", e=E), ones[:],
                          picked_before[:].unsqueeze(1).broadcast_to([P, NT, E]), start=False, stop=False)
                for back in range(1, NT):
                    last = pe.matmul(ranks[:, back * E:], ones[:], flat[:, 0:(NT - back) * E], start=False,
                                     stop=(back == NT - 1))
                last.then_inc(ranked, 1)

            def attend_and_route(a, b):
                if b is not None:
                    pe.wait_ge(slots_ready, b + FREE)
                if a is not None:
                    turn_tokens(a, x_ln, xn_ready, x_turned)
                    if b is not None:
                        pe.wait_ge(x2_made, b * 2 + 2)
                    scores(a)
                if b is not None:
                    turn_tokens(b, xn2, xn2_ready, x2_turned)
                    pe.wait_ge(x2t_split, b * 2 + 1)
                if a is not None:
                    turn_exps(a, 0)
                if b is not None:
                    pe.wait_ge(x2t_split, b * 2 + 2)
                    router_logits(b)
                    pe.wait_ge(logits_read, b + 1)
                if a is not None:
                    turn_exps(a, 1)
                    attention(a)
                if b is not None:
                    rank_tokens(b)

            attend_and_route(0, None)
            with pe.Fori(0, NB - 1) as i:
                attend_and_route(i + 1, i)
            attend_and_route(None, NB - 1)

            pe.wait_ge(slots_ready, NB + FREE)
            pe.matmul(ranks[:, 0:E], ones[:], picked_before[:], start=True, stop=True).then_inc(counted, 1)

            def w_g(odd, k, h):
                o = k * F + h * FH
                return [w[odd][:, o:o + FH] for w in (w_hi, w_lo)]

            def w_u(odd, k, h):
                o = KC * F + k * F + h * FH
                return [w[odd][:, o:o + FH] for w in (w_hi, w_lo)]

            def w_d(odd, c):
                o = 2 * KC * F + c * D
                return [w[odd][:, o:o + D] for w in (w_hi, w_lo)]

            def gate_up(odd, h, blk):
                pe.wait_ge(h_made[h], blk + FREE)
                if h == 0:
                    pe.wait_ge(bt_split, blk + 1 + FREE)
                for k in range(KC):
                    g, u = w_g(odd, k, h), w_u(odd, k, h)
                    first, last = k == 0, k == KC - 1
                    hi, lo = xt_hi[:, k, :], xt_lo[:, k, :]
                    pe.matmul(g_ps[h], hi, g[0], start=first, stop=False)
                    pe.matmul(g_ps[h], hi, g[1], start=False, stop=False)
                    pe.matmul(u_ps[h], hi, u[0], start=first, stop=False)
                    pe.matmul(u_ps[h], hi, u[1], start=False, stop=False)
                    pe.matmul(g_ps[h], lo, g[0], start=False, stop=last)
                    mm = pe.matmul(u_ps[h], lo, u[0], start=False, stop=last)
                mm.then_inc(gu_done[h], 1)

            def turn_h(h, blk):
                pe.wait_ge(h_made[h], blk + 1 + FREE)
                pe.wait_ge(ht_split[h], blk + FREE)
                for c in range(FC // 2):
                    mm = pe.transpose(ht_ps[h][:, c * P:(c + 1) * P], h_sb[h][:, c * P:(c + 1) * P], ident[:])
                mm.then_inc(h_turned[h], 1)

            def turn_x(blk):
                pe.wait_ge(block_loaded, blk * 16 + 16)
                pe.wait_ge(bt_split, blk + FREE)
                for k in range(KC):
                    mm = pe.transpose(xt_ps[:, k * P:(k + 1) * P], block_rows[:, k * P:(k + 1) * P], ident[:])
                mm.then_inc(block_turned, 1)

            def down(odd, h, blk):
                pe.wait_ge(ht_split[h], blk + 1 + FREE)
                if h == 0:
                    pe.wait_ge(y_weighted, blk + FREE)
                for c in range(FC // 2):
                    mm = product(y_ps, [t[h][:, c, :] for t in (ht_hi, ht_lo)], w_d(odd, h * (FC // 2) + c),
                                 h == 0 and c == 0, h == 1 and c == FC // 2 - 1)
                if h == 1:
                    mm.then_inc(y_done, 1)

            def inner_block(odd, blk):
                gate_up(odd, 0, blk + 1)
                turn_h(1, blk)
                turn_x(blk + 2)
                down(odd, 0, blk)
                gate_up(odd, 1, blk + 1)
                down(odd, 1, blk)
                turn_h(0, blk + 1)

            pe.wait_ge(plan_ready, 1)
            pe.wait_ge(first_split, 1)
            turn_x(0)
            with pe.Fori(0, E // 2) as pair:
                for odd in range(2):
                    e = pair * 2 + odd
                    n = pe.value_load(last_row[0:1, bass.ds(e, 1)], min_val=MIN_BLOCKS - 1, max_val=T // P - 1)
                    b0 = pe.value_load(first_row[0:1, bass.ds(e, 1)], min_val=0, max_val=T)
                    pe.wait_ge(w_split, e * PIECES + FREE)
                    gate_up(odd, 0, b0)
                    turn_x(b0 + 1)
                    gate_up(odd, 1, b0)
                    turn_h(0, b0)
                    inner_block(odd, b0)
                    with pe.Fori(1, n) as j:
                        inner_block(odd, b0 + j)
                    turn_h(1, b0 + n)
                    down(odd, 0, b0 + n)
                    down(odd, 1, b0 + n)


DVE_STEPS = 65

_INS = ['x', 'ctx_t', 'w_small', 'mask', 'bq', 'bk', 'bv', 'gates', 'wr_t', 'w_experts']


def kernel(x, ctx_1024, mask_BxS2_ik0, g_xattn, g_ffn, L0_xattn_Wq, L0_xattn_bq, L0_xattn_Wk, L0_xattn_bk,
           L0_xattn_Wv, L0_xattn_bv, L0_ffn_Wr, L0_ffn_Wg, L0_ffn_Wu, L0_ffn_Wd):
    import numpy as np
    import concourse.bacc as bacc
    from concourse.bass_utils import run_bass_kernel_spmd

    def by_partition(a):
        a = np.asarray(a)
        return a.reshape(a.shape[0] // P, P, -1).transpose(1, 0, 2)

    def chunks(a):
        return by_partition(a).reshape(P, -1)

    ctx_t = np.asarray(ctx_1024).transpose(2, 0, 1).reshape(D, NB * LC)
    small = [chunks(ctx_t), chunks(L0_xattn_Wk), chunks(L0_xattn_Wv), chunks(np.asarray(L0_xattn_Wq).T)]
    experts = np.empty((E, P, WCOLS), np.float32)
    for e in range(E):
        experts[e] = np.concatenate([chunks(np.asarray(L0_ffn_Wg)[e].T), chunks(np.asarray(L0_ffn_Wu)[e].T),
                                     chunks(np.asarray(L0_ffn_Wd)[e].T)], axis=1)
    arrays = {
        'x': np.asarray(x).reshape(T, D),
        'w_small': np.concatenate(small, axis=1),
        'mask': np.asarray(mask_BxS2_ik0).reshape(NB * LC),
        'bq': np.asarray(L0_xattn_bq).reshape(KC, P).T,
        'bk': np.asarray(L0_xattn_bk).reshape(KC, P).T,
        'bv': np.asarray(L0_xattn_bv),
        'gates': np.concatenate([np.asarray(g_xattn), np.asarray(g_ffn)]),
        'wr_t': chunks(np.asarray(L0_ffn_Wr).T),
        'w_experts': experts,
    }
    nc = bacc.Bacc("TRN2", target_bir_lowering=False, num_devices=1)
    arrays = {f"in_{k}": np.ascontiguousarray(v) for k, v in arrays.items()}
    aps = {k[3:]: nc.dram_tensor(k, v.shape, mybir.dt.from_np(v.dtype), kind="ExternalInput").ap()
           for k, v in arrays.items()}
    out = nc.dram_tensor("out_padded", (T + P, D), F32, kind="ExternalOutput").ap()
    build(nc, ctx_t=None, out=out, **aps)
    r = run_bass_kernel_spmd(nc, [arrays], core_ids=[0])
    return r.results[0]["out_padded"][0:T].reshape(NB, S, D)
```

```python
from contextlib import ExitStack

import concourse.bass as bass
from concourse import mybir

ALU = mybir.AluOpType
ACT = mybir.ActivationFunctionType
AX = mybir.AxisListType
F32 = mybir.dt.float32
F32R = mybir.dt.float32r
BF16 = mybir.dt.bfloat16
I32 = mybir.dt.int32

P = 128
NB, S, D = 4, 1024, 256
T = NB * S
LC = 154
CH = LC // 2
KC = D // P
NT = S // P
TQ = NT // 2
E, F = 8, 1024
FC = F // P
Q = 4
FQ = FC // Q
WCOLS = 2 * KC * F + FC * D
PIECE = 1024
PIECES = WCOLS // PIECE
PIECE_AFTER = [slice(0, 1), slice(1, 2), slice(0, 0), slice(2, 3)]
HALVES = 2
B = HALVES * P
MIN_BLOCKS = 3
REGION = T + B
ROW = D + 2 * E
LN_EPS = 1e-5
K_EPS = 2.0 ** -23
SCATTERED = 16 * 2 * TQ
FREE = 1
MASKED = -1e9 * 16.0
BELOW = -1e30


class Steps:

    def __init__(self, engine, sem):
        self.engine, self.sem, self.base, self.n = engine, sem, 0, 0

    def mark(self, ins):
        ins.then_inc(self.sem, 1)
        self.n += 1

    def settle(self):
        self.engine.wait_ge(self.sem, self.base + self.n)

    def loop(self, i, per):
        self.base, self.per, self.entry = self.n + i * per, per, self.n
        self.n = 0

    def leave(self, turns):
        assert self.n == self.per, (self.n, self.per)
        self.base, self.n = 0, self.entry + turns * self.per


def build(nc, x, w_small, mask, bq, bk, bv, gates, wr_t, w_experts, out):
    rows_dram = nc.dram_tensor("rows_by_expert", [E * REGION, ROW], F32).ap()

    with ExitStack() as whole:
        def sb(name, shape, dt, stack=whole):
            return stack.enter_context(nc.sbuf_tensor(name, shape, dt))

        def sem(name):
            return whole.enter_context(nc.semaphore(name))

        ps = whole.enter_context(nc.psum_tensor("ps", [P, 8, 512], F32))

        w_raw = sb("w_raw", [P, WCOLS], F32)
        w_hi = [sb("w_hi0", [P, WCOLS], F32R)]
        w_lo = [sb("w_lo0", [P, WCOLS], F32R)]
        ident = sb("ident", [P, P], F32)
        earlier = sb("earlier", [P, P], BF16)
        ones = sb("ones", [P, P], BF16)
        gate = sb("gate", [P, 2], F32)
        count_row = sb("count_row", [P, E], I32)
        last_row = sb("last_row", [P, E], I32)
        slots_i = sb("slots_i", [P, 2 * NT], I32)
        block_rows = sb("block_rows", [P, HALVES, D], F32)
        early_row = sb("early_row", [P, 1], I32)
        both_row = sb("both_row", [P, E], I32)
        first_row = sb("first_row", [P, E], I32)
        pads = sb("pads", [P, 2, HALVES, ROW], F32)

        att = ExitStack()
        x_ln = sb("x_ln", [P, NT, D], F32, att)
        t_hi = [sb(f"t_hi{q}", [P, KC, TQ * P], F32R, att) for q in range(2)]
        t_lo = [sb(f"t_lo{q}", [P, KC, TQ * P], F32R, att) for q in range(2)]
        m_hi = sb("m_hi", [P, KC * NB * LC + D - LC], F32R, att)
        m_lo = sb("m_lo", [P, KC * NB * LC + D - LC], F32R, att)
        v_hi = sb("v_hi", [P, NB * 2 * D], F32R, att)
        v_lo = sb("v_lo", [P, NB * 2 * D], F32R, att)
        wr_f = sb("wr_f", [P, KC, E], F32, att)
        wr_pair = sb("wr_pair", [P, KC, 2, E], F32R, att)
        bias_all = sb("bias_all", [P, NB * LC], F32, att)
        bias_now = sb("bias_now", [P, LC], F32, att)
        gate_in = sb("gate_in", [P, 2], F32, att)
        iota_i = sb("iota_i", [P, 2, E], I32, att)
        falling = sb("falling", [P, E], F32, att)
        region0 = sb("region0", [P, E], F32, att)
        stats = [sb(f"stats{n}", [P, NT, 6], F32, att) for n in range(2)]
        moments = [sb(f"moments{n}", [P, NT, 2], F32, att) for n in range(2)]
        ln_v = [sb(f"ln_v{n}", [P, NT], F32, att) for n in range(2)]
        ln_l = [sb(f"ln_l{n}", [P, NT], F32, att) for n in range(2)]
        ln_y = [sb(f"ln_y{n}", [P, NT], F32, att) for n in range(2)]
        ln_a = [sb(f"ln_a{n}", [P, NT], F32, att) for n in range(2)]
        ln_b = [sb(f"ln_b{n}", [P, NT], F32, att) for n in range(2)]
        rstd = [sb(f"rstd{n}", [P, NT], F32, att) for n in range(2)]
        shift = [sb(f"shift{n}", [P, NT], F32, att) for n in range(2)]
        neg_max = sb("neg_max", [P, NT], F32, att)
        exp_sum = sb("exp_sum", [P, NT], F32, att)
        exp_inv = sb("exp_inv", [P, NT], F32, att)
        att_scale = sb("att_scale", [P, NT], F32, att)
        logits = sb("logits", [P, NT, E], F32, att)
        logits_t = sb("logits_t", [2 * E, 2, TQ * P], F32, att)
        below = sb("below", [P, NT, E], F32, att)
        ex = sb("ex", [P, NT, E], F32, att)
        cand = sb("cand", [P, NT, E], F32, att)
        best = sb("best", [P, NT], F32, att)
        second = sb("second", [P, NT], F32, att)
        ratio = sb("ratio", [P, NT], F32, att)
        chosen = sb("chosen", [P, 2, NT, E], F32, att)
        slot_of = sb("slot_of", [P, 2, NT, E], F32, att)
        place = sb("place", [P, NT, E], F32, att)
        next_slot = sb("next_slot", [P, NT, E], F32, att)
        e_sum = sb("e_sum", [P, NT], F32, att)
        den = sb("den", [P, NT], F32, att)
        w_first = sb("w_first", [P, NT], F32, att)
        w_second = sb("w_second", [P, NT], F32, att)
        picked = sb("picked", [P, NT, E], BF16, att)
        picked_before = sb("picked_before", [P, E], BF16, att)
        picked_now = sb("picked_now", [P, E], F32, att)
        slots = sb("slots", [P, 2 * NT], F32, att)
        count_f = sb("count_f", [P, E], F32, att)
        blocks_i = sb("blocks_i", [P, E], I32, att)
        block_f = sb("block_f", [P, E], F32, att)
        running = [sb(f"running{n}", [P, 4 + E], F32, att) for n in range(2)]
        behind = sb("behind", [P, E], F32, att)
        pad_id = sb("pad_id", [P, HALVES, E], I32, att)

        prep = ExitStack()
        prep_in = sb("prep_in", [P, KC * NB * LC + 3 * KC * D], F32, prep)
        prep_hi = sb("prep_hi", [P, KC * NB * LC + 3 * KC * D], F32R, prep)
        prep_lo = sb("prep_lo", [P, KC * NB * LC + 3 * KC * D], F32R, prep)
        k_f = sb("k_f", [P, KC, NB * LC], F32, prep)
        k_hi = sb("k_hi", [P, KC, NB * LC], F32R, prep)
        k_lo = sb("k_lo", [P, KC, NB * LC], F32R, prep)
        v_f = sb("v_f", [P, NB * 2 * D], F32, prep)
        mask_i = sb("mask_i", [P, NB * LC], I32, prep)
        keep = sb("keep", [P, NB * LC], F32, prep)
        masked = sb("masked", [P, NB * LC], F32, prep)
        bias_cols = sb("bias_cols", [P, 2, KC], F32, prep)
        bq_hi = sb("bq_hi", [P, KC, P], F32R, prep)
        bq_lo = sb("bq_lo", [P, KC, P], F32R, prep)
        bv_row = sb("bv_row", [P, D], F32, prep)
        prep.close()
        sc = sb("sc", [P, NT, LC], F32, att)
        p_hi = [sb(f"p_hi{q}", [P, 2, TQ * P], F32R, att) for q in range(2)]
        p_lo = [sb(f"p_lo{q}", [P, 2, TQ * P], F32R, att) for q in range(2)]
        x_res = sb("x_res", [P, NT, D], F32, att)
        x2 = sb("x2", [P, NT, D], F32, att)
        xn2 = sb("xn2", [P, NT, D], F32, att)
        rows = sb("rows", [P, NT, ROW], F32, att)
        att.close()

        w_hi.append(sb("w_hi1", [P, WCOLS], F32R))
        w_lo.append(sb("w_lo1", [P, WCOLS], F32R))
        xt_hi = sb("xt_hi", [P, KC, B], F32R)
        xt_lo = sb("xt_lo", [P, KC, B], F32R)
        u_sb = [sb(f"u_sb{n}", [P, FQ, B], F32) for n in range(2)]
        ht = [sb(f"ht{q}", [P, FQ, B], F32) for q in range(Q)]
        ht_hi = [sb(f"ht_hi{q}", [P, FQ, B], F32R) for q in range(Q)]
        ht_lo = [sb(f"ht_lo{q}", [P, FQ, B], F32R) for q in range(Q)]
        weight_token = sb("weight_token", [P, HALVES, 2], F32)
        y_sb = sb("y_sb", [P, HALVES, D], F32)

        turned = [ps[:, 4 * q:4 * q + 2, :] for q in range(2)]
        prods = [ps[:, 4 * q + 2:4 * q + 4, :] for q in range(2)]
        logits_ps = turned[1][:, 0, 0:NT * 2 * E].rearrange("p (t two e) -> p t two e", two=2, e=E)
        logits_t_ps = turned[1][0:2 * E]
        ranks = prods[0][:, 0, 0:NT * E]
        g_ps = [ps[:, n, :].rearrange("p (c t) -> p c t", c=FQ) for n in range(2)]
        u_ps = [ps[:, 2 + n, :].rearrange("p (c t) -> p c t", c=FQ) for n in range(2)]
        xt_ps = ps[:, 4, :].rearrange("p (k t) -> p k t", k=KC)
        y_ps = ps[:, 6:8, 0:D]

        pool_waited = sem("pool_waited")
        dve_waited = sem("dve_waited")
        pe_waited = sem("pe_waited")
        sp_waited = sem("sp_waited")
        prep_loaded = [sem(f"prep_loaded{n}") for n in range(2)]
        small_loaded = sem("small_loaded")
        x_loaded = sem("x_loaded")
        x_res_loaded = sem("x_res_loaded")
        raw_loaded = [sem(f"raw_loaded{n}") for n in range(2)]
        consts_made = sem("consts_made")
        pool_step = sem("pool_step")
        dve_step = sem("dve_step")
        act_step = sem("act_step")
        prep_split_hi = sem("prep_split_hi")
        prep_split = sem("prep_split")
        wr_split_hi = sem("wr_split_hi")
        k_made = sem("k_made")
        k_masked = sem("k_masked")
        k_split_hi = sem("k_split_hi")
        k_split = sem("k_split")
        v_made = sem("v_made")
        v_biased = sem("v_biased")
        v_split_hi = sem("v_split_hi")
        v_split = sem("v_split")
        zeros_made = sem("zeros_made")
        exps_zeroed = sem("exps_zeroed")
        m_made = sem("m_made")
        m_split_hi = sem("m_split_hi")
        m_split = sem("m_split")
        bqk_made = sem("bqk_made")
        first_split = sem("first_split")
        var_ready = [sem(f"var_ready{n}") for n in range(2)]
        guess_ready = [sem(f"guess_ready{n}") for n in range(2)]
        rstd_ready = [sem(f"rstd_ready{n}") for n in range(2)]
        xn_ready = [sem(f"xn_ready{q}") for q in range(2)]
        x_turned = sem("x_turned")
        xt_split_hi = sem("xt_split_hi")
        xt_split = sem("xt_split")
        scored = sem("scored")
        maxed = sem("maxed")
        exped = sem("exped")
        p_turned = sem("p_turned")
        pt_split_hi = sem("pt_split_hi")
        pt_split = sem("pt_split")
        attended = sem("attended")
        x2_made = sem("x2_made")
        x2_stored = sem("x2_stored")
        xn2_ready = [sem(f"xn2_ready{q}") for q in range(2)]
        x2_turned = sem("x2_turned")
        x2t_split_hi = sem("x2t_split_hi")
        x2t_split = sem("x2t_split")
        logits_t_ready = sem("logits_t_ready")
        logits_t_read = sem("logits_t_read")
        logits_ready = sem("logits_ready")
        logits_read = sem("logits_read")
        rows_free = sem("rows_free")
        rows_filled = sem("rows_filled")
        below_ready = sem("below_ready")
        second_ready = sem("second_ready")
        route_exped = sem("route_exped")
        picked_ready = sem("picked_ready")
        ranked = sem("ranked")
        ranks_read = sem("ranks_read")
        slots_ready = sem("slots_ready")
        rows_scattered = [sem(f"rows_scattered{q}") for q in range(2)]
        counted = sem("counted")
        early_ready = sem("early_ready")
        plan_ready = sem("plan_ready")
        pads_ready = sem("pads_ready")
        pads_stored = sem("pads_stored")
        regions_filled = sem("regions_filled")
        dummy_stored = sem("dummy_stored")
        block_loaded = sem("block_loaded")
        block_turned = sem("block_turned")
        bt_split_hi = sem("bt_split_hi")
        bt_split = sem("bt_split")
        gu_done = [sem(f"gu_done{q}") for q in range(Q)]
        u_copied = [sem(f"u_copied{q}") for q in range(Q)]
        h_made = [sem(f"h_made{q}") for q in range(Q)]
        h_split_hi = [sem(f"h_split_hi{q}") for q in range(Q)]
        h_split = [sem(f"h_split{q}") for q in range(Q)]
        w_split_hi = sem("w_split_hi")
        w_split = sem("w_split")
        y_done = sem("y_done")
        y_weighted = sem("y_weighted")
        meta_loaded = sem("meta_loaded")
        y_added = sem("y_added")
        y_free = sem("y_free")

        ctx_hi = prep_hi[:, 0:KC * NB * LC].rearrange("p (k n) -> p k n", k=KC)
        ctx_lo = prep_lo[:, 0:KC * NB * LC].rearrange("p (k n) -> p k n", k=KC)

        first_cols = KC * NB * LC + KC * D
        prep_cols = [slice(0, first_cols), slice(first_cols, KC * NB * LC + 3 * KC * D)]

        def small_w(t, n):
            o = KC * NB * LC + n * KC * D
            return t[:, o:o + KC * D].rearrange("p (k n) -> p k n", k=KC)

        x_v = x.rearrange("(b p t) d -> b p (t d)", p=P, t=NT)
        out_v = out[0:T, :].rearrange("(b p t) d -> b p (t d)", p=P, t=NT)
        block = whole.enter_context(nc.Block())

        @block.sync
        def _(sp):
            flat = lambda t: t[:].rearrange("p t d -> p (t d)")

            def load_raw(src, half):
                cols = slice(half * WCOLS // 2, (half + 1) * WCOLS // 2)
                sp.dma_start(w_raw[:, cols], src[:, cols]).then_inc(raw_loaded[half], 16)

            for n in range(2):
                sp.dma_start(prep_in[:, prep_cols[n]], w_small[:, prep_cols[n]]).then_inc(prep_loaded[n], 16)
            sp.dma_start(mask_i[:], mask.partition_broadcast(P)).then_inc(small_loaded, 16)
            sp.dma_start(bias_cols[:, 0, :], bq).then_inc(small_loaded, 16)
            sp.dma_start(bias_cols[:, 1, :], bk).then_inc(small_loaded, 16)
            sp.dma_start(bv_row[:], bv.partition_broadcast(P)).then_inc(small_loaded, 16)
            sp.dma_start(gate_in[:], gates.partition_broadcast(P)).then_inc(small_loaded, 16)
            sp.dma_start(wr_f[:].rearrange("p k e -> p (k e)"), wr_t).then_inc(small_loaded, 16)
            sp.dma_start(flat(x_ln), x_v[0]).then_inc(x_loaded, 16)
            load_raw(w_experts[0], 0)
            load_raw(w_experts[0], 1)
            sp.wait_ge(pads_ready, 1)
            sp.dma_start(out[T:T + B, :].rearrange("(s p) d -> p s d", p=P), pads[:, :, 0, 0:D]
                         ).then_inc(dummy_stored, 16)
            sp.wait_ge(v_split, 1)
            sp.dma_start(flat(x_res), x_v[0]).then_inc(x_res_loaded, 16)
            sp.wait_ge(x_turned, 2)
            sp.dma_start(flat(x_ln), x_v[1]).then_inc(x_loaded, 16)

            for e in range(E):
                sp.dma_start(rows_dram[e * REGION:e * REGION + MIN_BLOCKS * B, :].rearrange(
                    "(n p k) c -> p n (k c)", p=P, k=HALVES),
                    pads[:, 1].rearrange("p k c -> p (k c)").unsqueeze(1).broadcast_to(
                        [P, MIN_BLOCKS, HALVES * ROW])).then_inc(regions_filled, 16)

            def store_x2(b):
                sp.wait_ge(x2_made, b * 2 + 2)
                sp.sem_inc(sp_waited)
                sp.dma_start(out_v[bass.ds(b, 1)].squeeze(0), flat(x2)).then_inc(x2_stored, 16)

            def load_res(b):
                sp.dma_start(flat(x_res), x_v[bass.ds(b, 1)].squeeze(0)).then_inc(x_res_loaded, 16)

            with sp.Fori(0, NB - 2) as i:
                store_x2(i)
                sp.wait_ge(x_turned, i * 2 + 4)
                sp.sem_inc(sp_waited)
                sp.dma_start(flat(x_ln), x_v[bass.ds(i + 2, 1)].squeeze(0)).then_inc(x_loaded, 16)
                load_res(i + 1)
            store_x2(NB - 2)
            load_res(NB - 1)
            store_x2(NB - 1)

            sp.wait_ge(first_split, 1)
            load_raw(w_experts[1], 0)
            load_raw(w_experts[1], 1)

            sp.wait_ge(early_ready, 1)
            early = sp.value_load(early_row[0:1, 0:1], min_val=0, max_val=T)

            def load_block(row, blk):
                sp.wait_ge(block_turned, blk + FREE)
                sp.sem_inc(sp_waited)
                sp.dma_start(block_rows[:], rows_dram[bass.ds(row, B), 0:D].rearrange("(a p) d -> p a d", p=P)
                             ).then_inc(block_loaded, 16)

            def load_first_blocks():
                load_block(0, 0)
                load_block(B, 1)

            with sp.If(early > 2 * B - 1):
                for q in range(2):
                    sp.wait_ge(rows_scattered[q], SCATTERED * (NB - 1))
                sp.sem_inc(sp_waited)
                load_first_blocks()

            sp.wait_ge(plan_ready, 1)
            for e in range(E):
                n = sp.value_load(count_row[0:1, e:e + 1], min_val=0, max_val=T)
                at = n + e * REGION
                sp.dma_start(rows_dram[bass.ds(at, B), :].rearrange("(p k) c -> p (k c)", p=P),
                             pads[:, 0].rearrange("p k c -> p (k c)")).then_inc(pads_stored, 16)
            sp.wait_ge(pads_stored, 16 * E)
            for q in range(2):
                sp.wait_ge(rows_scattered[q], SCATTERED * NB)
            sp.sem_inc(sp_waited)
            with sp.If(early < 2 * B):
                load_first_blocks()

            def load_expert(e, more, start=1):
                n = sp.value_load(last_row[0:1, bass.ds(e, 1)], min_val=MIN_BLOCKS - 1, max_val=T // B - 1)
                b0 = sp.value_load(first_row[0:1, bass.ds(e, 1)], min_val=0, max_val=T)
                with sp.Fori(start, n + 1) as j:
                    load_block(e * REGION + j * B, b0 + j)
                load_block(((e + 1) & (E - 1)) * REGION, b0 + n + 1)
                if more:
                    after = w_experts[bass.ds(e + 2, 1)].squeeze(0)
                    sp.wait_ge(w_split, e * PIECES + PIECES + FREE)
                    sp.sem_inc(sp_waited)
                    for half in range(2):
                        load_raw(after, half)

            load_expert(0, True, start=2)
            with sp.Fori(1, E - 2) as e:
                load_expert(e, True)
            with sp.Fori(E - 2, E) as e:
                load_expert(e, False)
            for half in range(2):
                sp.wait_ge(raw_loaded[half], 16 * E)
            sp.wait_ge(x_loaded, 16 * NB)
            sp.wait_ge(x_res_loaded, 16 * NB)
            sp.wait_ge(x2_stored, 16 * NB)
            sp.wait_ge(dummy_stored, 16)

        @block.gpsimd
        def _(pool):
            step = Steps(pool, pool_step)
            for s in (*h_made, *h_split, ranks_read, block_turned, bt_split, w_split, y_done, y_weighted,
                      y_free):
                pool.sem_inc(s, FREE)
            pool.memset(ident[:], 0.0)
            pool.memset(earlier[:], 1.0)
            pool.memset(ones[:], 1.0)
            pool.memset(picked_before[:], 0.0)
            pool.iota(iota_i[:, 0, :], [[-1, E]], base=E, channel_multiplier=0)
            pool.iota(iota_i[:, 1, :], [[REGION, E]], base=0, channel_multiplier=0)
            pool.iota(pad_id[:], [[1, HALVES], [0, E]], base=0, channel_multiplier=HALVES)
            row_words = rows[:, :, D:ROW].bitcast(I32).rearrange("p t (e two) -> p t e two", two=2)[:, :, :, 1]
            step.mark(pool.memset(pads[:], 0.0))
            step.settle()
            pool.affine_select(out=ident[:], in_=ident[:], compare_op=ALU.not_equal, fill=1.0, base=0,
                               pattern=[[-1, P]], channel_multiplier=1)
            pool.affine_select(out=earlier[:], in_=earlier[:], compare_op=ALU.is_gt, fill=0.0, base=0,
                               pattern=[[1, P]], channel_multiplier=-1).then_inc(consts_made, 1)

            for c in range(PIECES):
                if c % (PIECES // 2) == 0:
                    pool.wait_ge(raw_loaded[c // (PIECES // 2)], 16)
                cols = slice(c * PIECE, (c + 1) * PIECE)
                step.mark(pool.tensor_scalar(w_hi[0][:, cols], w_raw[:, cols], 1.0, None, ALU.mult))
            step.settle()
            for c in range(PIECES):
                cols = slice(c * PIECE, (c + 1) * PIECE)
                last = pool.tensor_tensor(w_lo[0][:, cols], w_raw[:, cols], w_hi[0][:, cols].bitcast(F32),
                                          ALU.subtract)
            last.then_inc(first_split, 1)

            pool.wait_ge(v_split, 1)
            step.mark(pool.iota(row_words, [[1, NT], [0, E]], base=-S, channel_multiplier=NT))
            step.settle()

            def number_rows():
                step.mark(pool.tensor_scalar(row_words, row_words, float(S), None, ALU.add))
                step.settle()
                pool.sem_inc(rows_free)

            def scatter(b):
                pool.wait_ge(slots_ready, b + 1)
                pool.wait_ge(rows_filled, b + 1)
                pool.sem_inc(pool_waited)
                for q in range(2):
                    for t in range(q * TQ, (q + 1) * TQ):
                        for k in range(2):
                            pool.indirect_dma_start(
                                rows_dram,
                                bass.IndirectOffsetOnAxis(ap=slots_i[:, k * NT + t:k * NT + t + 1], axis=0),
                                rows[:, t, :], None).then_inc(rows_scattered[q], 16)

            pool.wait_ge(regions_filled, 16 * E)
            number_rows()
            scatter(0)
            with pool.Fori(1, NB) as i:
                step.loop(i - 1, 1)
                for q in range(2):
                    pool.wait_ge(rows_scattered[q], i * SCATTERED)
                pool.sem_inc(pool_waited)
                number_rows()
                scatter(i)
            step.leave(NB - 1)

            pool.wait_ge(plan_ready, 1)
            pool.wait_ge(pads_stored, 16 * E)
            for q in range(2):
                pool.wait_ge(rows_scattered[q], SCATTERED * NB)
            pool.wait_ge(x2_stored, 16 * NB)
            pool.wait_ge(dummy_stored, 16)
            with pool.Fori(0, E) as e:
                n = pool.value_load(last_row[0:1, bass.ds(e, 1)], min_val=MIN_BLOCKS - 1, max_val=T // B - 1)
                b0 = pool.value_load(first_row[0:1, bass.ds(e, 1)], min_val=0, max_val=T)
                with pool.Fori(0, n + 1) as j:
                    pool.dma_start(weight_token[:],
                                   rows_dram[bass.ds(e * REGION + j * B, B), bass.ds(e * 2 + D, 2)].rearrange(
                                       "(a p) c -> p a c", p=P)).then_inc(meta_loaded, 16)
                    pool.wait_ge(meta_loaded, (b0 + j) * 16 + 16)
                    pool.wait_ge(y_weighted, b0 + j + 1 + FREE)
                    pool.sem_inc(pool_waited)
                    for a in range(HALVES):
                        pool.indirect_dma_start(
                            out, bass.IndirectOffsetOnAxis(ap=weight_token[:, a, 1:2].bitcast(I32), axis=0),
                            y_sb[:, a, :], None, compute_op=ALU.add).then_inc(y_added, 16)
                        pool.wait_ge(y_added, (b0 + j) * (16 * HALVES) + (16 * a + 16))
                        pool.sem_inc(pool_waited)
                    pool.sem_inc(y_free)

        @block.scalar
        def _(act):
            step = Steps(act, act_step)
            for n in range(2):
                act.wait_ge(prep_loaded[n], 16)
                act.copy(prep_hi[:, prep_cols[n]], prep_in[:, prep_cols[n]]).then_inc(prep_split_hi, 1)
            act.wait_ge(small_loaded, 16 * 6)
            act.copy(wr_pair[:, :, 0, :], wr_f[:]).then_inc(wr_split_hi, 1)
            step.mark(act.activation(gate[:], gate_in[:], ACT.Tanh))
            act.preload_act_table_set("natural_log_exp_and_others")
            pad_zeros = pads[:, 0, 0, :]
            act.wait_ge(consts_made, 1)
            for t in (m_hi, m_lo):
                act.copy(t[:, KC * NB * LC:], pad_zeros[:, 0:D - LC])
            for t in (v_hi, v_lo):
                last = act.copy(t[P // 2:P, :], pad_zeros[P // 2:P, 0:1].broadcast_to([P // 2, NB * 2 * D]))
            last.then_inc(zeros_made, 1)
            def guess_rstd(n, b):
                act.wait_ge(var_ready[n], b + 1)
                step.mark(act.activation(ln_l[n][:], ln_v[n][:], ACT.Ln))
                step.settle()
                act.activation(ln_y[n][:], ln_l[n][:], ACT.Exp, scale=-0.5).then_inc(guess_ready[n], 1)

            def normalise(n, b, qs, source, result, ready):
                act.wait_ge(rstd_ready[n], b + 1)
                for q in qs:
                    for t in range(q * TQ, (q + 1) * TQ):
                        last = act.activation(result[:, t, :], source[:, t, :], ACT.Identity,
                                              bias=shift[n][:, t:t + 1], scale=rstd[n][:, t:t + 1])
                    last.then_inc(ready[q], 1)

            def split_turned(b, qs, ready, result, rows_of, split):
                for q in qs:
                    act.wait_ge(ready, b * 2 + q + 1)
                    act.copy(result[q][0:rows_of], turned[q][0:rows_of]).then_inc(split, 1)

            def exps(b, q):
                act.wait_ge(maxed, b * 2 + q + 1)
                for t in range(q * TQ, (q + 1) * TQ):
                    last = act.activation(sc[:, t, :], sc[:, t, :], ACT.Exp, bias=neg_max[:, t:t + 1],
                                          scale=-1.0, accum_out=exp_sum[:, t:t + 1])
                last.then_inc(exped, 1)

            def route_exps(b):
                act.wait_ge(below_ready, b + 1)
                act.activation(ex[:], below[:], ACT.Exp)
                act.wait_ge(second_ready, b + 1)
                act.activation(ratio[:], second[:], ACT.Exp).then_inc(route_exped, 1)

            def fill_rows(b):
                act.wait_ge(rows_free, b + 1)
                act.wait_ge(xn2_ready[0], b + 1)
                act.copy(rows[:, :, 0:D], xn2[:]).then_inc(rows_filled, 1)

            def attend_and_route(a, b, l):
                if b is not None:
                    guess_rstd(1, b)
                    normalise(1, b, [1], x2, xn2, xn2_ready)
                if a is not None:
                    exps(a, 0)
                if b is not None:
                    split_turned(b, range(2), x2_turned, t_hi, P, x2t_split_hi)
                if a is not None:
                    exps(a, 1)
                    split_turned(a, [0], p_turned, p_hi, CH, pt_split_hi)
                if b is not None:
                    act.wait_ge(logits_t_ready, b + 1)
                    act.copy(logits_t[:], logits_t_ps).then_inc(logits_t_read, 1)
                    if l is not None:
                        guess_rstd(0, l)
                if a is not None:
                    split_turned(a, [1], p_turned, p_hi, CH, pt_split_hi)
                if l is not None:
                    if b is None:
                        guess_rstd(0, l)
                    normalise(0, l, [0], x_ln, x_ln, xn_ready)
                if b is not None:
                    route_exps(b)
                if l is not None:
                    normalise(0, l, [1], x_ln, x_ln, xn_ready)
                if l is not None:
                    split_turned(l, range(2), x_turned, t_hi, P, xt_split_hi)
                if b is not None:
                    fill_rows(b)

            guess_rstd(0, 0)
            act.wait_ge(k_masked, 1)
            act.copy(k_hi[:], k_f[:]).then_inc(k_split_hi, 1)
            act.wait_ge(m_made, 1)
            for m in range(KC):
                last = act.copy(m_hi[:, m * NB * LC:(m + 1) * NB * LC].rearrange("p (h n) -> p h n", h=2),
                                ps[:, 2 * m:2 * m + 2, 0:2 * LC])
            last.then_inc(m_split_hi, 1)
            normalise(0, 0, [1], x_ln, x_ln, xn_ready)
            act.wait_ge(v_biased, 1)
            act.wait_ge(zeros_made, 1)
            act.copy(v_hi[0:CH, :], v_f[0:CH, :]).then_inc(v_split_hi, 1)
            split_turned(0, range(2), x_turned, t_hi, P, xt_split_hi)
            act.wait_ge(v_split, 1)
            for t in (*p_hi, *p_lo):
                last = act.copy(t[P // 2:P].rearrange("p c t -> p (c t)"),
                                pad_zeros[P // 2:P, 0:1].broadcast_to([P // 2, 2 * TQ * P]))
            last.then_inc(exps_zeroed, 1)
            act.wait_ge(exps_zeroed, 1)
            attend_and_route(0, None, 1)
            with act.Fori(0, NB - 2) as i:
                step.loop(i, 2)
                attend_and_route(i + 1, i, i + 2)
            step.leave(NB - 2)
            attend_and_route(NB - 1, NB - 2, None)
            attend_and_route(None, NB - 1, None)

            act.wait_ge(plan_ready, 1)

            def piece(e, odd, c):
                cols = slice(c * PIECE, (c + 1) * PIECE)
                act.copy(w_hi[1 - odd][:, cols], w_raw[:, cols]).then_inc(w_split_hi, 1)

            def copy_u(q, blk):
                act.wait_ge(gu_done[q], blk + 1)
                act.copy(u_sb[q % 2][:], u_ps[q % 2]).then_inc(u_copied[q], 1)

            def split_h(q, blk):
                act.wait_ge(h_made[q], blk + 1 + FREE)
                act.copy(ht_hi[q][:], ht[q][:]).then_inc(h_split_hi[q], 1)

            def split_x(blk):
                act.wait_ge(block_turned, blk + 1 + FREE)
                act.copy(xt_hi[:], xt_ps).then_inc(bt_split_hi, 1)

            def one_block(blk, e=None, odd=None, pieces=()):
                for q in range(Q):
                    if q == Q - 1:
                        act.wait_ge(gu_done[q], blk + 1)
                        split_x(blk + 1)
                    copy_u(q, blk)
                    split_h(q, blk)
                    for c in pieces[PIECE_AFTER[q]]:
                        piece(e, odd, c)

            def expert(e, odd, first=False, last=False):
                n = act.value_load(last_row[0:1, bass.ds(e, 1)], min_val=MIN_BLOCKS - 1, max_val=T // B - 1)
                b0 = act.value_load(first_row[0:1, bass.ds(e, 1)], min_val=0 if first else MIN_BLOCKS, max_val=T)
                if last:
                    with act.Fori(0, n + 1) as j:
                        one_block(b0 + j)
                    return
                act.wait_ge(raw_loaded[0], e * 16 + 32)
                one_block(b0, e, odd, range(0, 3))
                act.wait_ge(raw_loaded[1], e * 16 + 32)
                if not first:
                    act.wait_ge(y_done, b0 + FREE)
                one_block(b0 + 1, e, odd, range(3, 6))
                with act.Fori(2, n + 1) as j:
                    one_block(b0 + j)

            split_x(0)
            expert(0, 0, first=True)
            with act.Fori(0, E // 2 - 1) as pair:
                expert(pair * 2 + 1, 1)
                expert(pair * 2 + 2, 0)
            expert(E - 1, 1, last=True)

        @block.vector
        def _(dve):
            step = Steps(dve, dve_step)
            for n in range(2):
                dve.wait_ge(prep_split_hi, n + 1)
                dve.tensor_tensor(prep_lo[:, prep_cols[n]], prep_in[:, prep_cols[n]],
                                  prep_hi[:, prep_cols[n]].bitcast(F32), ALU.subtract).then_inc(prep_split, 1)
            dve.wait_ge(small_loaded, 16 * 6)
            dve.wait_ge(consts_made, 1)
            dve.tensor_scalar(keep[:], mask_i[:], 0.0, None, ALU.not_equal)
            dve.tensor_copy(bq_hi[:], bias_cols[:, 0, :].unsqueeze(2).broadcast_to([P, KC, P]))
            dve.tensor_copy(falling[:], iota_i[:, 0, :])
            dve.tensor_copy(region0[:], iota_i[:, 1, :])
            dve.wait_ge(wr_split_hi, 1)
            dve.tensor_tensor(wr_pair[:, :, 1, :], wr_f[:], wr_pair[:, :, 0, :].bitcast(F32), ALU.subtract)
            step.mark(dve.tensor_scalar(pad_id[:], pad_id[:], P - 1, None, ALU.bitwise_and))
            step.settle()
            for kind in range(2):
                pad_words = pads[:, kind, :, D:ROW].bitcast(I32).rearrange("p k (e two) -> p k e two", two=2)
                last = dve.tensor_scalar(pad_words[:, :, :, 1], pad_id[:], float(T + kind * P), None, ALU.add)
            last.then_inc(pads_ready, 1)
            dve.tensor_scalar(masked[:], keep[:], -MASKED, MASKED, ALU.mult, ALU.add)
            step.mark(dve.tensor_tensor(bq_lo[:], bias_cols[:, 0, :].unsqueeze(2).broadcast_to([P, KC, P]),
                                        bq_hi[:].bitcast(F32), ALU.subtract))
            step.settle()
            def measure(n, q, source):
                for t in range(q * TQ, (q + 1) * TQ):
                    step.mark(dve.bn_stats(stats[n][:, t, :], source[:, t, :]))

            def find_variance(n):
                step.settle()
                dve.sem_inc(dve_waited)
                for t in range(NT):
                    step.mark(dve.bn_aggr(moments[n][:, t, :], stats[n][:, t, :]))
                step.settle()
                dve.tensor_scalar(ln_v[n][:], moments[n][:, :, 1], LN_EPS, None, ALU.add).then_inc(var_ready[n], 1)

            def newton(n, b):
                dve.wait_ge(guess_ready[n], b + 1)
                step.mark(dve.scalar_tensor_tensor(ln_a[n][:], ln_v[n][:], -0.5, ln_y[n][:], ALU.mult, ALU.mult))
                step.settle()
                step.mark(dve.tensor_tensor(ln_b[n][:], ln_a[n][:], ln_y[n][:], ALU.mult))
                step.settle()
                step.mark(dve.scalar_tensor_tensor(rstd[n][:], ln_b[n][:], 1.5, ln_y[n][:], ALU.add, ALU.mult))
                step.settle()
                dve.scalar_tensor_tensor(shift[n][:], moments[n][:, :, 0], -1.0, rstd[n][:], ALU.mult, ALU.mult
                                         ).then_inc(rstd_ready[n], 1)

            def normalise(n, b, source, result, ready):
                dve.wait_ge(rstd_ready[n], b + 1)
                for t in range(TQ):
                    last = dve.tensor_scalar(result[:, t, :], source[:, t, :], moments[n][:, t, 0:1],
                                             rstd[n][:, t:t + 1], ALU.subtract, ALU.mult)
                last.then_inc(ready[0], 1)

            def split_turned(b, q, split_hi, lo, hi, rows_of, split):
                dve.wait_ge(split_hi, b * 2 + q + 1)
                dve.tensor_tensor(lo[q][0:rows_of], turned[q][0:rows_of], hi[q][0:rows_of].bitcast(F32),
                                  ALU.subtract).then_inc(split, 1)

            def scores(b, q):
                if q == 0:
                    step.mark(dve.tensor_copy(bias_now[:], bias_all[:, bass.ds(b * LC, LC)]))
                    step.settle()
                dve.wait_ge(scored, b * 2 + q + 1)
                dve.sem_inc(dve_waited)
                for t in range(TQ):
                    last = dve.tensor_tensor_reduce(
                        out=sc[:, q * TQ + t, :], in0=prods[q][:, t // 2, (t % 2) * D:(t % 2) * D + LC],
                        in1=bias_now[:], scale=-float(D) ** -0.5, scalar=3e38, op0=ALU.add, op1=ALU.min,
                        accum_out=neg_max[:, q * TQ + t:q * TQ + t + 1])
                last.then_inc(maxed, 1)

            def scale_attention(b):
                dve.wait_ge(exped, b * 2 + 2)
                step.mark(dve.reciprocal(exp_inv[:], exp_sum[:]))
                step.settle()
                step.mark(dve.tensor_scalar(att_scale[:], exp_inv[:], gate[:, 0:1], None, ALU.mult))
                step.settle()

            def residual(b, q):
                if q == 0:
                    dve.wait_ge(x_res_loaded, b * 16 + 16)
                dve.wait_ge(attended, b * 2 + q + 1)
                for t in range(q * TQ, (q + 1) * TQ):
                    last = dve.scalar_tensor_tensor(
                        x2[:, t, :], prods[q][:, (t % TQ) // 2, (t % 2) * D:(t % 2 + 1) * D],
                        att_scale[:, t:t + 1], x_res[:, t, :], ALU.mult, ALU.add)
                last.then_inc(x2_made, 1)

            def read_logits(b):
                dve.wait_ge(logits_ready, b + 1)
                dve.tensor_reduce(logits[:], logits_ps.rearrange("p t two e -> p t e two"), AX.X, ALU.add
                                  ).then_inc(logits_read, 1)

            def choose_experts(b):
                lg = logits[:]
                fall = falling[:].unsqueeze(1).broadcast_to([P, NT, E])
                dve.wait_ge(logits_read, b + 1)
                step.mark(dve.tensor_reduce(best[:], lg, AX.X, ALU.max))
                step.settle()
                dve.tensor_tensor(below[:], lg, best[:].unsqueeze(2).broadcast_to([P, NT, E]), ALU.subtract
                                  ).then_inc(below_ready, 1)
                dve.wait_ge(below_ready, b + 1)

                def choose(k):
                    step.mark(dve.tensor_reduce(best[:], cand[:], AX.X, ALU.max))
                    step.settle()
                    step.mark(dve.tensor_tensor(chosen[:, k], cand[:],
                                                best[:].unsqueeze(2).broadcast_to([P, NT, E]), ALU.is_equal))
                    step.settle()

                step.mark(dve.scalar_tensor_tensor(cand[:], below[:], 0.0, fall, ALU.is_ge, ALU.mult))
                step.settle()
                choose(0)
                step.mark(dve.scalar_tensor_tensor(place[:].rearrange("p t e -> p (t e)"),
                                                   chosen[:, 0].rearrange("p t e -> p (t e)"), BELOW,
                                                   below[:].rearrange("p t e -> p (t e)"), ALU.mult, ALU.add))
                step.settle()
                dve.tensor_reduce(second[:], place[:], AX.X, ALU.max).then_inc(second_ready, 1)
                dve.wait_ge(second_ready, b + 1)
                step.mark(dve.tensor_tensor(cand[:], place[:], second[:].unsqueeze(2).broadcast_to([P, NT, E]),
                                            ALU.is_ge))
                step.settle()
                step.mark(dve.tensor_tensor(cand[:], cand[:], fall, ALU.mult))
                step.settle()
                choose(1)
                dve.tensor_tensor(picked[:], chosen[:, 0], chosen[:, 1], ALU.add).then_inc(picked_ready, 1)

            def weigh_choice(b):
                dve.wait_ge(route_exped, b + 1)
                step.mark(dve.tensor_reduce(e_sum[:], ex[:], AX.X, ALU.add))
                step.settle()
                step.mark(dve.scalar_tensor_tensor(den[:], e_sum[:], K_EPS, ratio[:], ALU.mult, ALU.add))
                step.settle()
                step.mark(dve.tensor_scalar(den[:], den[:], 1.0, None, ALU.add))
                step.settle()
                step.mark(dve.reciprocal(w_first[:], den[:]))
                step.settle()
                step.mark(dve.tensor_tensor(w_second[:], w_first[:], ratio[:], ALU.mult))
                step.settle()
                dve.scalar_tensor_tensor(cand[:], chosen[:, 0], gate[:, 1:2],
                                         w_first[:].unsqueeze(2).broadcast_to([P, NT, E]), ALU.mult, ALU.mult)
                step.mark(dve.scalar_tensor_tensor(place[:], chosen[:, 1], gate[:, 1:2],
                                                   w_second[:].unsqueeze(2).broadcast_to([P, NT, E]),
                                                   ALU.mult, ALU.mult))
                step.settle()

            def read_ranks(b, last=False):
                dve.wait_ge(ranked, b + 1)
                dve.tensor_tensor(next_slot[:], ranks.rearrange("p (t e) -> p t e", e=E),
                                  region0[:].unsqueeze(1).broadcast_to([P, NT, E]), ALU.add
                                  ).then_inc(ranks_read, 1)
                if last:
                    dve.wait_ge(ranks_read, NB + FREE)
                    dve.tensor_copy(early_row[:], next_slot[:, 0, 0:1]).then_inc(early_ready, 1)

            def find_slots(b):
                dve.wait_ge(rows_free, b + 1)
                row_weights = rows[:, :, D:ROW].rearrange("p t (e two) -> p t e two", two=2)[:, :, :, 0]
                step.mark(dve.tensor_tensor(row_weights, cand[:], place[:], ALU.add))
                step.settle()
                dve.wait_ge(ranks_read, b + 1 + FREE)
                step.mark(dve.tensor_reduce(picked_now[:], picked[:].rearrange("p t e -> p e t"), AX.X, ALU.add))
                step.settle()
                step.mark(dve.tensor_tensor(slot_of[:, 0], chosen[:, 0], next_slot[:], ALU.mult))
                step.mark(dve.tensor_tensor(slot_of[:, 1], chosen[:, 1], next_slot[:], ALU.mult))
                step.mark(dve.tensor_tensor(picked_before[:], picked_before[:], picked_now[:], ALU.add))
                step.settle()
                step.mark(dve.tensor_reduce(slots[:], slot_of[:].rearrange("p k t e -> p (k t) e"), AX.X, ALU.add))
                step.settle()
                dve.tensor_copy(slots_i[:], slots[:]).then_inc(slots_ready, 1)

            def attend_and_route(a, b, l):
                def second_variance(b):
                    dve.wait_ge(x2_made, b * 2 + 2)
                    for q in range(2):
                        measure(1, q, x2)
                    find_variance(1)

                if b is not None and a is not None:
                    second_variance(b)
                if a is not None:
                    scores(a, 0)
                if b is not None:
                    newton(1, b)
                    normalise(1, b, x2, xn2, xn2_ready)
                if a is not None:
                    scores(a, 1)
                if b is not None:
                    if l is not None:
                        dve.wait_ge(x_loaded, l * 16 + 16)
                        measure(0, 0, x_ln)
                    for q in range(2):
                        split_turned(b, q, x2t_split_hi, t_lo, t_hi, P, x2t_split)
                    if l is not None:
                        measure(0, 1, x_ln)
                        find_variance(0)
                if a is not None:
                    split_turned(a, 0, pt_split_hi, p_lo, p_hi, CH, pt_split)
                    scale_attention(a)
                if b is not None:
                    read_logits(b)
                    if l is not None:
                        newton(0, l)
                    choose_experts(b)
                if a is not None:
                    split_turned(a, 1, pt_split_hi, p_lo, p_hi, CH, pt_split)
                if l is not None and b is None:
                    dve.wait_ge(x_loaded, l * 16 + 16)
                    for q in range(2):
                        measure(0, q, x_ln)
                    find_variance(0)
                    newton(0, l)
                if b is not None:
                    if a is not None:
                        dve.wait_ge(x2_stored, b * 16 + 16)
                        for q in range(2):
                            dve.wait_ge(xn2_ready[q], b + 1)
                if a is not None:
                    residual(a, 0)
                if b is not None:
                    weigh_choice(b)
                if a is not None:
                    residual(a, 1)
                    if l is None:
                        second_variance(a)
                if b is not None:
                    read_ranks(b, last=a is None)
                if l is not None:
                    for q in range(2):
                        split_turned(l, q, xt_split_hi, t_lo, t_hi, P, xt_split)
                if b is not None:
                    find_slots(b)

            dve.wait_ge(x_loaded, 16)
            for q in range(2):
                measure(0, q, x_ln)
            find_variance(0)
            dve.wait_ge(k_made, 1)
            for m in range(KC):
                for h in range(2):
                    cols = slice(h * 2 * LC, (h + 1) * 2 * LC)
                    last = dve.scalar_tensor_tensor(k_f[:, m, cols], ps[:, 2 * m + h, 0:2 * LC],
                                                    bias_cols[:, 1, m:m + 1], keep[:, cols], ALU.add, ALU.mult)
            last.then_inc(k_masked, 1)
            dve.wait_ge(k_split_hi, 1)
            dve.tensor_tensor(k_lo[:], k_f[:], k_hi[:].bitcast(F32), ALU.subtract).then_inc(k_split, 1)
            step.mark(dve.memset(picked_now[:], 0.0))
            newton(0, 0)
            dve.wait_ge(v_made, 1)
            dve.tensor_tensor(v_f[0:CH, :].rearrange("p (n d) -> p n d", d=D),
                              ps[0:CH, 4:8, :].rearrange("p k (n d) -> p (k n) d", d=D),
                              bv_row[0:CH, :].unsqueeze(1).broadcast_to([CH, 2 * NB, D]), ALU.add
                              ).then_inc(v_biased, 1)
            normalise(0, 0, x_ln, x_ln, xn_ready)
            dve.wait_ge(m_split_hi, 1)
            for m in range(KC):
                cols = slice(m * NB * LC, (m + 1) * NB * LC)
                dve.tensor_tensor(m_lo[:, cols].rearrange("p (h n) -> p h n", h=2),
                                  ps[:, 2 * m:2 * m + 2, 0:2 * LC],
                                  m_hi[:, cols].bitcast(F32).rearrange("p (h n) -> p h n", h=2), ALU.subtract)
            dve.wait_ge(bqk_made, 1)
            dve.tensor_tensor(bias_all[:].rearrange("p (h n) -> p h n", h=2), ps[:, 4:6, 0:2 * LC],
                              masked[:].rearrange("p (h n) -> p h n", h=2), ALU.add).then_inc(m_split, 1)
            for q in range(2):
                split_turned(0, q, xt_split_hi, t_lo, t_hi, P, xt_split)
            dve.wait_ge(v_split_hi, 1)
            dve.tensor_tensor(v_lo[0:CH, :], v_f[0:CH, :], v_hi[0:CH, :].bitcast(F32), ALU.subtract
                              ).then_inc(v_split, 1)
            dve.wait_ge(v_split, 1)
            attend_and_route(0, None, 1)
            with dve.Fori(0, NB - 2) as i:
                step.loop(i, DVE_STEPS)
                attend_and_route(i + 1, i, i + 2)
            step.leave(NB - 2)
            attend_and_route(NB - 1, NB - 2, None)
            attend_and_route(None, NB - 1, None)

            for t in running:
                step.mark(dve.memset(t[:], 0.0))
            step.settle()
            dve.wait_ge(counted, 1)
            dve.tensor_copy(count_row[:], ranks[:, 0:E])
            step.mark(dve.tensor_scalar(blocks_i[:], ranks[:, 0:E], float(B - 1), None, ALU.add))
            step.settle()
            step.mark(dve.tensor_scalar(blocks_i[:], blocks_i[:], B.bit_length() - 1, None,
                                        ALU.logical_shift_right))
            step.settle()
            step.mark(dve.tensor_scalar(block_f[:], blocks_i[:], float(MIN_BLOCKS), None, ALU.max))
            step.mark(dve.tensor_scalar(running[0][:, 5:4 + E], blocks_i[:, 0:E - 1], float(MIN_BLOCKS), None, ALU.max))
            step.settle()
            step.mark(dve.tensor_tensor(running[1][:, 4:], running[0][:, 4:], running[0][:, 3:3 + E], ALU.add))
            dve.tensor_scalar(last_row[:], block_f[:], -1.0, None, ALU.add)
            step.mark(dve.scalar_tensor_tensor(behind[:], block_f[:], -float(B), ranks[:, 0:E], ALU.mult, ALU.add))
            step.settle()
            step.mark(dve.tensor_tensor(running[0][:, 4:], running[1][:, 4:], running[1][:, 2:2 + E], ALU.add))
            dve.tensor_scalar(both_row[:], behind[:], float(-P), None, ALU.is_gt)
            step.settle()
            dve.tensor_tensor(first_row[:], running[0][:, 4:], running[0][:, 0:E], ALU.add).then_inc(plan_ready, 1)
            dve.wait_ge(plan_ready, 1)

            def piece(e, odd, c):
                cols = slice(c * PIECE, (c + 1) * PIECE)
                dve.wait_ge(w_split_hi, e * PIECES + (c + 1))
                dve.tensor_tensor(w_lo[1 - odd][:, cols], w_raw[:, cols], w_hi[1 - odd][:, cols].bitcast(F32),
                                  ALU.subtract).then_inc(w_split, 1)

            def make_h(q, blk):
                dve.wait_ge(u_copied[q], blk + 1)
                dve.scalar_tensor_tensor(ht[q][:], g_ps[q % 2], 0.0, u_sb[q % 2][:], ALU.max, ALU.mult
                                         ).then_inc(h_made[q], 1)

            def split_h(q, blk):
                dve.wait_ge(h_split_hi[q], blk + 1)
                dve.tensor_tensor(ht_lo[q][:], ht[q][:], ht_hi[q][:].bitcast(F32), ALU.subtract
                                  ).then_inc(h_split[q], 1)

            def split_x(blk):
                dve.wait_ge(bt_split_hi, blk + 1)
                dve.tensor_tensor(xt_lo[:], xt_ps, xt_hi[:].bitcast(F32), ALU.subtract).then_inc(bt_split, 1)

            def weigh_y(blk):
                dve.wait_ge(y_done, blk + 1 + FREE)
                dve.wait_ge(meta_loaded, blk * 16 + 16)
                dve.wait_ge(y_free, blk + FREE)
                for a in range(HALVES):
                    last = dve.tensor_scalar(y_sb[:, a, :], y_ps[:, a], weight_token[:, a, 0:1], None, ALU.mult)
                last.then_inc(y_weighted, 1)

            def one_block(blk, e=None, odd=None, pieces=(), start=False):
                for q in range(Q):
                    if q == Q - 1:
                        split_x(blk + 1)
                    make_h(q, blk)
                    split_h(q, blk)
                    if q == 1 and not start:
                        weigh_y(blk - 1)
                    for c in pieces[PIECE_AFTER[q]]:
                        piece(e, odd, c)

            def expert(e, odd, first=False, last=False):
                n = dve.value_load(last_row[0:1, bass.ds(e, 1)], min_val=MIN_BLOCKS - 1, max_val=T // B - 1)
                b0 = dve.value_load(first_row[0:1, bass.ds(e, 1)], min_val=0 if first else MIN_BLOCKS, max_val=T)
                if last:
                    with dve.Fori(0, n + 1) as j:
                        one_block(b0 + j)
                    weigh_y(b0 + n)
                    return
                one_block(b0, e, odd, range(0, 3), start=first)
                one_block(b0 + 1, e, odd, range(3, 6))
                with dve.Fori(2, n + 1) as j:
                    one_block(b0 + j)

            split_x(0)
            expert(0, 0, first=True)
            with dve.Fori(0, E // 2 - 1) as pair:
                expert(pair * 2 + 1, 1)
                expert(pair * 2 + 2, 0)
            expert(E - 1, 1, last=True)

        @block.tensor
        def _(pe):
            def product(o, lhs, rhs, first, last):
                pe.matmul(o, lhs[0], rhs[0], start=first, stop=False)
                pe.matmul(o, lhs[0], rhs[1], start=False, stop=False)
                return pe.matmul(o, lhs[1], rhs[0], start=False, stop=last)

            wk = [small_w(t, 0) for t in (prep_hi, prep_lo)]
            wv = [small_w(t, 1) for t in (prep_hi, prep_lo)]
            wq = [small_w(t, 2) for t in (prep_hi, prep_lo)]
            ctx = [ctx_hi, ctx_lo]
            kk = [k_hi, k_lo]
            pe.wait_ge(prep_split, 1)
            for m in range(KC):
                for h in range(2):
                    for k in range(KC):
                        last = product(ps[:, 2 * m + h, 0:2 * LC], [w[:, k, m * P:(m + 1) * P] for w in wk],
                                       [c[:, k, h * 2 * LC:(h + 1) * 2 * LC] for c in ctx], k == 0, k == KC - 1)
            last.then_inc(k_made, 1)
            pe.wait_ge(prep_split, 2)
            for n in range(2 * NB):
                for k in range(KC):
                    last = product(ps[0:CH, 4 + n // 2, (n % 2) * D:(n % 2 + 1) * D],
                                   [c[:, k, n * CH:(n + 1) * CH] for c in ctx], [w[:, k, :] for w in wv],
                                   k == 0, k == KC - 1)
            last.then_inc(v_made, 1)
            pe.wait_ge(k_split, 1)
            for m in range(KC):
                for h in range(2):
                    for k in range(KC):
                        last = product(ps[:, 2 * m + h, 0:2 * LC], [w[:, k, m * P:(m + 1) * P] for w in wq],
                                       [t[:, k, h * 2 * LC:(h + 1) * 2 * LC] for t in kk], k == 0, k == KC - 1)
            last.then_inc(m_made, 1)
            pe.wait_ge(v_biased, 1)
            for h in range(2):
                for k in range(KC):
                    last = product(ps[:, 4 + h, 0:2 * LC], [t[:, k, :] for t in (bq_hi, bq_lo)],
                                   [t[:, k, h * 2 * LC:(h + 1) * 2 * LC] for t in kk], k == 0, k == KC - 1)
            last.then_inc(bqk_made, 1)
            pe.wait_ge(m_split, 1)
            pe.wait_ge(consts_made, 1)

            tt = [[t_hi[q], t_lo[q]] for q in range(2)]

            def turn_tokens(b, source, ready, done):
                for q in range(2):
                    pe.wait_ge(ready[q], b + 1)
                    for k in range(KC):
                        for t in range(TQ):
                            last = pe.transpose(turned[q][:, k, t * P:(t + 1) * P],
                                                source[:, q * TQ + t, k * P:(k + 1) * P], ident[:])
                    last.then_inc(done, 1)

            def scores(b):
                for q in range(2):
                    pe.wait_ge(xt_split, b * 2 + q + 1)
                    for t in range(TQ):
                        for k in range(KC):
                            last = product(prods[q][:, t // 2, (t % 2) * D:(t % 2 + 1) * D],
                                           [a[:, k, t * P:(t + 1) * P] for a in tt[q]],
                                           [m[:, bass.ds(b * LC + k * NB * LC, D)] for m in (m_hi, m_lo)],
                                           k == 0, k == KC - 1)
                    last.then_inc(scored, 1)

            def turn_exps(b, q):
                pe.wait_ge(exped, b * 2 + q + 1)
                for c in range(2):
                    for t in range(TQ):
                        last = pe.transpose(turned[q][0:CH, c, t * P:(t + 1) * P],
                                            sc[:, q * TQ + t, c * CH:(c + 1) * CH], ident[:])
                last.then_inc(p_turned, 1)

            def attention(b, q):
                pe.wait_ge(pt_split, b * 2 + q + 1)
                for t in range(TQ):
                    for c in range(2):
                        last = product(prods[q][:, t // 2, (t % 2) * D:(t % 2 + 1) * D],
                                       [a[:, c, t * P:(t + 1) * P] for a in (p_hi[q], p_lo[q])],
                                       [v[:, bass.ds(b * (2 * D) + c * D, D)] for v in (v_hi, v_lo)],
                                       c == 0, c == 1)
                last.then_inc(attended, 1)

            def router_logits(b):
                pe.wait_ge(x2t_split, b * 2 + 2)
                for q in range(2):
                    for k in range(KC):
                        pe.matmul(logits_t_ps[:, q], wr_pair[:, k].rearrange("p two e -> p (two e)"),
                                  t_hi[q][:, k, :], start=k == 0, stop=False)
                        last = pe.matmul(logits_t_ps[0:E, q], wr_pair[:, k, 0, :], t_lo[q][:, k, :],
                                         start=False, stop=k == KC - 1)
                last.then_inc(logits_t_ready, 1)

            def turn_logits(b):
                pe.wait_ge(logits_t_read, b + 1)
                pe.sem_inc(pe_waited)
                for t in range(NT):
                    last = pe.transpose(logits_ps[:, t].rearrange("p two e -> p (two e)"),
                                        logits_t[:, t // TQ, (t % TQ) * P:(t % TQ + 1) * P],
                                        ident[0:2 * E, 0:2 * E])
                last.then_inc(logits_ready, 1)

            def rank_tokens(b):
                pe.wait_ge(picked_ready, b + 1)
                flat = picked[:].rearrange("p t e -> p (t e)")
                pe.matmul(ranks, earlier[:], flat, start=True, stop=False)
                pe.matmul(ranks.rearrange("p (t e) -> p t e", e=E), ones[:],
                          picked_before[:].unsqueeze(1).broadcast_to([P, NT, E]), start=False, stop=False)
                for back in range(1, NT):
                    last = pe.matmul(ranks[:, back * E:], ones[:], flat[:, 0:(NT - back) * E], start=False,
                                     stop=(back == NT - 1))
                last.then_inc(ranked, 1)

            def attend_and_route(a, b, l):
                if a is not None:
                    if b is not None:
                        pe.wait_ge(ranks_read, b + FREE)
                        pe.wait_ge(x2_made, b * 2 + 2)
                    scores(a)
                if b is not None:
                    turn_tokens(b, xn2, xn2_ready, x2_turned)
                if a is not None:
                    if b is not None:
                        pe.wait_ge(x2t_split, b * 2 + 1)
                    turn_exps(a, 0)
                if b is not None:
                    router_logits(b)
                    turn_logits(b)
                if a is not None:
                    if b is not None:
                        pe.wait_ge(logits_read, b + 1)
                    turn_exps(a, 1)
                    attention(a, 0)
                    attention(a, 1)
                if l is not None:
                    turn_tokens(l, x_ln, xn_ready, x_turned)
                if b is not None:
                    if a is not None:
                        pe.wait_ge(x2_made, b * 2 + 3)
                    else:
                        pe.wait_ge(ranks_read, b + FREE)
                    rank_tokens(b)

            turn_tokens(0, x_ln, xn_ready, x_turned)
            attend_and_route(0, None, 1)
            with pe.Fori(0, NB - 2) as i:
                attend_and_route(i + 1, i, i + 2)
            attend_and_route(NB - 1, NB - 2, None)
            attend_and_route(None, NB - 1, None)

            pe.wait_ge(slots_ready, NB)
            pe.matmul(ranks[:, 0:E], ones[:], picked_before[:], start=True, stop=True).then_inc(counted, 1)

            def gate_up(odd, q, blk):
                pe.wait_ge(h_made[(q + 2) % Q], (blk if q < 2 else blk + 1) + FREE)
                if q == 0:
                    pe.wait_ge(bt_split, blk + 1 + FREE)
                for up, bank in enumerate((g_ps[q % 2], u_ps[q % 2])):
                    for c in range(FQ):
                        for k in range(KC):
                            o = (up * KC + k) * F + (q * FQ + c) * P
                            mm = product(bank[:, c], [w[odd][:, o:o + P] for w in (w_hi, w_lo)],
                                         [xt_hi[:, k, :], xt_lo[:, k, :]], k == 0, k == KC - 1)
                mm.then_inc(gu_done[q], 1)

            def turn_x(blk):
                pe.wait_ge(block_loaded, blk * 16 + 16)
                pe.wait_ge(bt_split, blk + FREE)
                for k in range(KC):
                    for a in range(HALVES):
                        mm = pe.transpose(xt_ps[:, k, a * P:(a + 1) * P], block_rows[:, a, k * P:(k + 1) * P],
                                          ident[:])
                mm.then_inc(block_turned, 1)

            def down_half(odd, q, a, c):
                o = 2 * KC * F + (q * FQ + c) * D
                return product(y_ps[:, a], [t[q][:, c, a * P:(a + 1) * P] for t in (ht_hi, ht_lo)],
                               [w[odd][:, o:o + D] for w in (w_hi, w_lo)],
                               q == 0 and c == 0, q == Q - 1 and c == FQ - 1)

            def down(odd, q, blk, both=None):
                pe.wait_ge(h_split[q], blk + 1 + FREE)
                if q == 0:
                    pe.wait_ge(y_weighted, blk + FREE)
                down_half(odd, q, 0, 0)
                if both is None:
                    for c in range(FQ):
                        down_half(odd, q, 1, c)
                else:
                    with pe.If(both > 0):
                        for c in range(FQ):
                            down_half(odd, q, 1, c)
                mm = down_half(odd, q, 0, 1)
                if q == Q - 1:
                    mm.then_inc(y_done, 1)

            def one_block(before, odd, blk, both_before=None, both=None):
                gate_up(odd, 0, blk)
                if before is not None:
                    down(before, 2, blk - 1, both_before)
                gate_up(odd, 1, blk)
                turn_x(blk + 1)
                if before is not None:
                    down(before, 3, blk - 1, both_before)
                gate_up(odd, 2, blk)
                gate_up(odd, 3, blk)
                down(odd, 0, blk, both)
                down(odd, 1, blk, both)

            def expert(e, odd, first=False):
                n = pe.value_load(last_row[0:1, bass.ds(e, 1)], min_val=MIN_BLOCKS - 1, max_val=T // B - 1)
                b0 = pe.value_load(first_row[0:1, bass.ds(e, 1)], min_val=0 if first else MIN_BLOCKS, max_val=T)
                both_before = None if first else pe.value_load(both_row[0:1, bass.ds(e - 1, 1)], min_val=0, max_val=1)
                if not first:
                    pe.wait_ge(w_split, e * PIECES + FREE)
                one_block(None if first else 1 - odd, odd, b0, both_before)
                with pe.Fori(1, n) as j:
                    one_block(odd, odd, b0 + j)
                both = pe.value_load(both_row[0:1, bass.ds(e, 1)], min_val=0, max_val=1)
                one_block(odd, odd, b0 + n, both=both)
                return b0 + n, both

            turn_x(0)
            pe.wait_ge(plan_ready, 1)
            pe.wait_ge(first_split, 1)
            expert(0, 0, first=True)
            with pe.Fori(0, E // 2 - 1) as pair:
                expert(pair * 2 + 1, 1)
                expert(pair * 2 + 2, 0)
            end, both = expert(E - 1, 1)
            down(1, 2, end, both)
            down(1, 3, end, both)


DVE_STEPS = 62


def kernel(x, ctx_1024, mask_BxS2_ik0, g_xattn, g_ffn, L0_xattn_Wq, L0_xattn_bq, L0_xattn_Wk, L0_xattn_bk,
           L0_xattn_Wv, L0_xattn_bv, L0_ffn_Wr, L0_ffn_Wg, L0_ffn_Wu, L0_ffn_Wd):
    import numpy as np
    import concourse.bacc as bacc
    from concourse.bass_utils import run_bass_kernel_spmd

    def by_partition(a):
        a = np.asarray(a)
        return a.reshape(a.shape[0] // P, P, -1).transpose(1, 0, 2)

    def chunks(a):
        return by_partition(a).reshape(P, -1)

    ctx_t = np.asarray(ctx_1024).transpose(2, 0, 1).reshape(D, NB * LC)
    small = [chunks(ctx_t), chunks(L0_xattn_Wk), chunks(L0_xattn_Wv), chunks(np.asarray(L0_xattn_Wq).T)]
    experts = np.empty((E, P, WCOLS), np.float32)
    for e in range(E):
        experts[e] = np.concatenate([chunks(np.asarray(L0_ffn_Wg)[e].T), chunks(np.asarray(L0_ffn_Wu)[e].T),
                                     chunks(np.asarray(L0_ffn_Wd)[e].T)], axis=1)
    arrays = {
        'x': np.asarray(x).reshape(T, D),
        'w_small': np.concatenate(small, axis=1),
        'mask': np.asarray(mask_BxS2_ik0).reshape(NB * LC),
        'bq': np.asarray(L0_xattn_bq).reshape(KC, P).T,
        'bk': np.asarray(L0_xattn_bk).reshape(KC, P).T,
        'bv': np.asarray(L0_xattn_bv),
        'gates': np.concatenate([np.asarray(g_xattn), np.asarray(g_ffn)]),
        'wr_t': chunks(np.asarray(L0_ffn_Wr).T),
        'w_experts': experts,
    }
    nc = bacc.Bacc("TRN2", target_bir_lowering=False, num_devices=1)
    arrays = {f"in_{k}": np.ascontiguousarray(v) for k, v in arrays.items()}
    aps = {k[3:]: nc.dram_tensor(k, v.shape, mybir.dt.from_np(v.dtype), kind="ExternalInput").ap()
           for k, v in arrays.items()}
    out = nc.dram_tensor("out_padded", (T + B, D), F32, kind="ExternalOutput").ap()
    build(nc, out=out, **aps)
    r = run_bass_kernel_spmd(nc, [arrays], core_ids=[0])
    return r.results[0]["out_padded"][0:T].reshape(NB, S, D)
```
